# Optimizing a Trainium2 kernel written in Bass

```python
import numpy as np
import jax
import jax.numpy as jnp

def _softmax(x, axis=-1):
    return jax.nn.softmax(x, axis=axis)

def _gelu(x):
    return jax.nn.gelu(x, approximate=True)

def _silu(x):
    return jax.nn.silu(x)

def _sigmoid(x):
    return jax.nn.sigmoid(x)

def _layernorm(x, axis=-1, eps=1e-05):
    m = jnp.mean(x, axis=axis, keepdims=True)
    v = jnp.var(x, axis=axis, keepdims=True)
    return (x - m) / jnp.sqrt(v + eps)

def _scatter_add(tgt, idx, src, axis=0):
    return tgt.at[idx].add(src)

def _segment_sum(src, seg, n):
    return jax.ops.segment_sum(src, seg, n)
kernel_name = 'mk_seq_preln_d1_jaxref_r8_ccb9d7'

def setup_inputs(seed: int=0):
    np.random.seed(seed)
    _w = jnp.asarray

    def _L0_attn_setup():
        import jax, jax.numpy as jnp
        import numpy as np
        B, S, D = (2, 512, 256)
        H, HKV, DH = (16, 4, 128)
        CHUNK = 64
        GROUPS = H // HKV

        def _alibi_slopes(n_heads):
            i = jnp.arange(1, n_heads + 1, dtype=jnp.float32)
            return jnp.exp2(-8.0 * i / n_heads)

        def _rope(x):
            s, d = (x.shape[2], x.shape[3])
            inv_freq = 1.0 / 10000.0 ** (jnp.arange(0, d, 2, dtype=jnp.float32) / d)
            freqs = jnp.arange(s, dtype=jnp.float32)[:, None] * inv_freq[None, :]
            cos = jnp.concatenate([jnp.cos(freqs), jnp.cos(freqs)], axis=-1)
            sin = jnp.concatenate([jnp.sin(freqs), jnp.sin(freqs)], axis=-1)
            x1, x2 = (x[..., :d // 2], x[..., d // 2:])
            rot = jnp.concatenate([-x2, x1], axis=-1)
            return x * cos[None, None] + rot * sin[None, None]

        def _lightning_attn(q, k, v):
            b, h, s, dh = q.shape
            nc = s // CHUNK
            lam = _alibi_slopes(h)
            r = jnp.arange(CHUNK, dtype=jnp.float32)
            diff = r[:, None] - r[None, :]
            diag = jnp.where(diff >= 0, jnp.exp(-lam[:, None, None] * diff), 0.0)
            q_dec = jnp.exp(-lam[:, None] * (r + 1.0))
            k_dec = jnp.exp(-lam[:, None] * (CHUNK - 1.0 - r))
            blk = jnp.exp(-lam * CHUNK)
            qc = q.reshape(b, h, nc, CHUNK, dh).transpose(2, 0, 1, 3, 4)
            kc = k.reshape(b, h, nc, CHUNK, dh).transpose(2, 0, 1, 3, 4)
            vc = v.reshape(b, h, nc, CHUNK, dh).transpose(2, 0, 1, 3, 4)

            def step(kv, inp):
                qi, ki, vi = inp
                scores = jnp.einsum('bhid,bhjd->bhij', qi, ki) * diag[None]
                o_intra = jnp.einsum('bhij,bhje->bhie', scores, vi)
                o_inter = jnp.einsum('bhid,bhde->bhie', qi * q_dec[None, :, :, None], kv)
                kv = blk[None, :, None, None] * kv + jnp.einsum('bhjd,bhje->bhde', ki * k_dec[None, :, :, None], vi)
                return (kv, o_intra + o_inter)
            kv0 = jnp.zeros((b, h, dh, dh), q.dtype)
            _, o = jax.lax.scan(step, kv0, (qc, kc, vc))
            return o.transpose(1, 2, 0, 3, 4).reshape(b, h, s, dh)
        key = jax.random.key(seed)
        ks = jax.random.split(key, 5)
        sc = 0.02
        return {'x': jax.random.normal(ks[0], (B, S, D), jnp.float32), 'wq': jax.random.normal(ks[1], (H * DH, D), jnp.float32) * sc, 'wk': jax.random.normal(ks[2], (HKV * DH, D), jnp.float32) * sc, 'wv': jax.random.normal(ks[3], (HKV * DH, D), jnp.float32) * sc, 'wo': jax.random.normal(ks[4], (D, H * DH), jnp.float32) * sc}
    _L0_attn_in = _L0_attn_setup()

    def _L0_ffn_setup():
        import jax, jax.numpy as jnp
        import numpy as np
        B, S, D, H = (4, 256, 256, 1024)

        def fwht(x):
            orig_shape = x.shape
            n = orig_shape[-1]
            x = x.reshape(-1, n)
            h = 1
            while h < n:
                xb = x.reshape(-1, n // (2 * h), 2, h)
                a = xb[:, :, 0, :]
                b = xb[:, :, 1, :]
                x = jnp.stack([a + b, a - b], axis=2).reshape(-1, n)
                h *= 2
            scale = jnp.asarray(1.0 / np.sqrt(n), dtype=x.dtype)
            return (x * scale).reshape(orig_shape)
        key = jax.random.key(seed)
        kx, k1, k2, k3 = jax.random.split(key, 4)
        x = jax.random.normal(kx, (B, S, D), dtype=jnp.float32)
        W1 = jax.random.normal(k1, (H, D), dtype=jnp.float32) * (1.0 / np.sqrt(D))
        W2 = jax.random.normal(k2, (D, H), dtype=jnp.float32) * (1.0 / np.sqrt(H))
        W3 = jax.random.normal(k3, (H, D), dtype=jnp.float32) * (1.0 / np.sqrt(D))
        return {'x': x, 'W1': W1, 'W2': W2, 'W3': W3}
    _L0_ffn_in = _L0_ffn_setup()
    _d = {'L0_attn_x': _L0_attn_in['x'], 'L0_attn_wq': _L0_attn_in['wq'], 'L0_attn_wk': _L0_attn_in['wk'], 'L0_attn_wv': _L0_attn_in['wv'], 'L0_attn_wo': _L0_attn_in['wo'], 'L0_ffn_W1': _L0_ffn_in['W1'], 'L0_ffn_W2': _L0_ffn_in['W2'], 'L0_ffn_W3': _L0_ffn_in['W3']}
    _x0 = _d['L0_attn_x']
    _d['L0_attn_x'] = jax.random.normal(jax.random.fold_in(jax.random.key(seed), 1), (4, 256, 256), dtype=_x0.dtype)
    del _x0
    return _d

def reference(L0_attn_x, L0_attn_wq, L0_attn_wk, L0_attn_wv, L0_attn_wo, L0_ffn_W1, L0_ffn_W2, L0_ffn_W3):

    def _L0_attn_ref(x, wq, wk, wv, wo):
        import jax, jax.numpy as jnp
        import numpy as np
        B, S, D = (2, 512, 256)
        H, HKV, DH = (16, 4, 128)
        CHUNK = 64
        GROUPS = H // HKV

        def _alibi_slopes(n_heads):
            i = jnp.arange(1, n_heads + 1, dtype=jnp.float32)
            return jnp.exp2(-8.0 * i / n_heads)

        def _rope(x):
            s, d = (x.shape[2], x.shape[3])
            inv_freq = 1.0 / 10000.0 ** (jnp.arange(0, d, 2, dtype=jnp.float32) / d)
            freqs = jnp.arange(s, dtype=jnp.float32)[:, None] * inv_freq[None, :]
            cos = jnp.concatenate([jnp.cos(freqs), jnp.cos(freqs)], axis=-1)
            sin = jnp.concatenate([jnp.sin(freqs), jnp.sin(freqs)], axis=-1)
            x1, x2 = (x[..., :d // 2], x[..., d // 2:])
            rot = jnp.concatenate([-x2, x1], axis=-1)
            return x * cos[None, None] + rot * sin[None, None]

        def _lightning_attn(q, k, v):
            b, h, s, dh = q.shape
            nc = s // CHUNK
            lam = _alibi_slopes(h)
            r = jnp.arange(CHUNK, dtype=jnp.float32)
            diff = r[:, None] - r[None, :]
            diag = jnp.where(diff >= 0, jnp.exp(-lam[:, None, None] * diff), 0.0)
            q_dec = jnp.exp(-lam[:, None] * (r + 1.0))
            k_dec = jnp.exp(-lam[:, None] * (CHUNK - 1.0 - r))
            blk = jnp.exp(-lam * CHUNK)
            qc = q.reshape(b, h, nc, CHUNK, dh).transpose(2, 0, 1, 3, 4)
            kc = k.reshape(b, h, nc, CHUNK, dh).transpose(2, 0, 1, 3, 4)
            vc = v.reshape(b, h, nc, CHUNK, dh).transpose(2, 0, 1, 3, 4)

            def step(kv, inp):
                qi, ki, vi = inp
                scores = jnp.einsum('bhid,bhjd->bhij', qi, ki) * diag[None]
                o_intra = jnp.einsum('bhij,bhje->bhie', scores, vi)
                o_inter = jnp.einsum('bhid,bhde->bhie', qi * q_dec[None, :, :, None], kv)
                kv = blk[None, :, None, None] * kv + jnp.einsum('bhjd,bhje->bhde', ki * k_dec[None, :, :, None], vi)
                return (kv, o_intra + o_inter)
            kv0 = jnp.zeros((b, h, dh, dh), q.dtype)
            _, o = jax.lax.scan(step, kv0, (qc, kc, vc))
            return o.transpose(1, 2, 0, 3, 4).reshape(b, h, s, dh)
        b, s, _ = x.shape
        q = jnp.einsum('bsd,ed->bse', x, wq).reshape(b, s, H, DH).transpose(0, 2, 1, 3)
        k = jnp.einsum('bsd,ed->bse', x, wk).reshape(b, s, HKV, DH).transpose(0, 2, 1, 3)
        v = jnp.einsum('bsd,ed->bse', x, wv).reshape(b, s, HKV, DH).transpose(0, 2, 1, 3)
        q = _rope(q)
        k = _rope(k)
        k = jnp.repeat(k, GROUPS, axis=1)
        v = jnp.repeat(v, GROUPS, axis=1)
        o = _lightning_attn(q, k, v)
        o = o.transpose(0, 2, 1, 3).reshape(b, s, H * DH)
        return jnp.einsum('bse,de->bsd', o, wo)

    def _L0_ffn_ref(x, W1, W2, W3):
        import jax, jax.numpy as jnp
        import numpy as np
        B, S, D, H = (4, 256, 256, 1024)

        def fwht(x):
            orig_shape = x.shape
            n = orig_shape[-1]
            x = x.reshape(-1, n)
            h = 1
            while h < n:
                xb = x.reshape(-1, n // (2 * h), 2, h)
                a = xb[:, :, 0, :]
                b = xb[:, :, 1, :]
                x = jnp.stack([a + b, a - b], axis=2).reshape(-1, n)
                h *= 2
            scale = jnp.asarray(1.0 / np.sqrt(n), dtype=x.dtype)
            return (x * scale).reshape(orig_shape)
        up_gate = jnp.einsum('bsd,hd->bsh', x, W1)
        up_lin = jnp.einsum('bsd,hd->bsh', x, W3)
        hidden = jax.nn.silu(up_gate) * up_lin
        hidden = fwht(hidden)
        out = jnp.einsum('bsh,dh->bsd', hidden, W2)
        return out
    x = L0_attn_x
    x = x + _L0_attn_ref(_layernorm(x, axis=-1), L0_attn_wq, L0_attn_wk, L0_attn_wv, L0_attn_wo)
    x = x + _L0_ffn_ref(_layernorm(x, axis=-1), L0_ffn_W1, L0_ffn_W2, L0_ffn_W3)
    return x

_drawn_inputs = setup_inputs


def setup_inputs(seed=0):
    import zlib

    import numpy as np

    out = dict(_drawn_inputs(seed))
    spreads = {}
    factors = {}
    for name, (base, spread) in spreads.items():
        noise = np.random.default_rng([zlib.crc32(name.encode()), seed]).standard_normal(out[name].shape)
        drawn = base * np.exp(spread * noise) if base else spread * noise
        out[name] = jnp.asarray(drawn.astype(out[name].dtype))
    for name, factor in factors.items():
        out[name] = (out[name] * factor).astype(out[name].dtype)
    return out
```

```python
from contextlib import ExitStack

import numpy as np

import concourse.bass as bass
from concourse import mybir

F32 = mybir.dt.float32
F32R = mybir.dt.float32r
ALU = mybir.AluOpType
ACT = mybir.ActivationFunctionType

P = 128
D = 256
KD = D // P
SEQ = 256
NSEQ = 4
HALVES = 2
TOK = NSEQ * SEQ // HALVES
BH = TOK // SEQ
TT = TOK // P
HEADS = 16
KVH = 4
PAIRS = HEADS // 2
PPG = PAIRS // KVH
HID = 1024
HT = HID // P
EPS = 1e-5
UNITS = HALVES * PAIRS

CH = 1024
AT_K, AT_V, AT_Q, AT_O = 0, CH, 2 * CH, 6 * CH
W_COLS = 10 * CH
AT_W2 = AT_K
AT_FF = AT_Q
CHUNKS = ([("wk", 0, AT_K), ("wv", 0, AT_V), ("wq", 0, AT_Q), ("wo", 0, AT_O)]
          + [(w, i, at + i * CH) for i in range(1, 4) for w, at in (("wq", AT_Q), ("wo", AT_O))]
          + [("w1", 0, AT_FF), ("w3", 0, AT_FF + CH), ("w1", 1, AT_FF + 2 * CH), ("w3", 1, AT_FF + 3 * CH)]
          + [("w2", 0, None), ("w2", 1, None)])
CHUNK_NO = {(w, i): n for n, (w, i, _) in enumerate(CHUNKS)}
SPLIT_CHUNKS = CHUNK_NO[("w2", 0)]


def lin_order():
    items = []
    for c in range(HALVES):
        items += [("X", c, k) for k in range(KD)] + [("K", c, 0)] + [("V", c, t) for t in range(TT)]
        items += [("Q", c, 0), ("Q", c, 1)]
        for p in range(PAIRS - 1):
            items += [("Q", c, 2 * p + 2), ("Q", c, 2 * p + 3)]
            if p % PPG == 0 and p // PPG + 1 < KVH:
                items.append(("K", c, p // PPG + 1))
    return items + [("X", HALVES, k) for k in range(KD)]


LIN = lin_order()
LIN_NO = {item: n for n, item in enumerate(LIN)}
ROPE_NO = {item: n for n, item in enumerate(i for i in LIN if i[0] in "KQ")}
V_NO = {item: n for n, item in enumerate(i for i in LIN if i[0] == "V")}
X_NO = {item: n for n, item in enumerate(i for i in LIN if i[0] == "X")}

S_FIRST0, S_SECOND, S_FIRST1 = range(3)
S_OF_SEQ = (S_FIRST0, S_FIRST1)
W2_TILES = 4


def step_rope(c, p):
    if p < PAIRS - 1:
        items = [("Q", c, 2 * p + 2), ("Q", c, 2 * p + 3)]
        if p % PPG == 0 and p // PPG + 1 < KVH:
            items.append(("K", c, p // PPG + 1))
        return items
    return []


def step_chunk(c, p):
    if c == 0:
        n = 4 + p
        return n if n < CHUNK_NO[("w1", 0)] else None
    return CHUNK_NO[("w1", 0)] + p // 2 if p % 2 == 1 else None


def build(nc, x, wk, wv, wq, wo, w1, w3, w2, cos, sin, decay, ident, hadamard, out):
    dram = {"wk": wk, "wv": wv, "wq": wq, "wo": wo, "w1": w1, "w3": w3, "w2": w2}

    with ExitStack() as ctx:
        def sb(name, shape, dt=F32):
            return ctx.enter_context(nc.sbuf_tensor(name, shape, dt))

        def sem(name):
            return ctx.enter_context(nc.semaphore(name))

        w_hi = sb("w_hi", [P, W_COLS], F32R)
        w_lo = sb("w_lo", [P, W_COLS], F32R)
        w_raw = sb("w_raw", [P, 2, CH])
        x_sb = sb("x_sb", [P, HALVES * TT, D])
        xn = sb("xn", [P, TT, D])
        xt_hi = sb("xt_hi", [P, KD, TOK], F32R)
        xt_lo = sb("xt_lo", [P, KD, TOK], F32R)
        k_hi = sb("k_hi", [P, 2, TOK], F32R)
        k_lo = sb("k_lo", [P, 2, TOK], F32R)
        v_hid = sb("v_hid", [P, 2, TT * KVH * P], F32R)
        q_hid = sb("q_hid", [P, 2, 2 * 2 * TOK], F32R)
        rope_a = sb("rope_a", [P, 2, TOK])
        rope_b = sb("rope_b", [P, 2, TOK])
        qk = sb("qk", [P, 2, TOK])
        p_raw = sb("p_raw", [P, 2, TOK])
        p_hi = sb("p_hi", [P, 3, TOK], F32R)
        p_lo = sb("p_lo", [P, 3, TOK], F32R)
        o_hi = sb("o_hi", [P, BH, 2, SEQ], F32R)
        o_lo = sb("o_lo", [P, BH, 2, SEQ], F32R)
        cos_sb = sb("cos_sb", [P, SEQ])
        sin_sb = sb("sin_sb", [P, SEQ])
        decay_sb = sb("decay_sb", [P, HEADS, SEQ])
        ident_sb = sb("ident_sb", [P, P])
        had_raw = sb("had_raw", [P, P])
        had = sb("had", [P, P], F32R)
        stats = sb("stats", [P, TT, 6])
        mean_var = sb("mean_var", [P, TT, 2])
        var_eps = sb("var_eps", [P, TT])
        rstd = sb("rstd", [P, TT])
        minus_half = sb("minus_half", [P, TT])

        bank = [ctx.enter_context(nc.psum_tensor(f"bank{i}", [P, 512], F32)) for i in range(8)]
        lin_bank = bank[0:2]
        s_bank = bank[2:5]
        o_bank = bank[5]
        y_bank = bank[6:8]
        up_bank = (bank[0:2], bank[2:4])
        t_bank = bank[4:6]
        down_bank = (bank[6], bank[7], bank[4], bank[5])

        v_hi = v_hid[:, 0, :].rearrange("p (t g e) -> p t g e", t=TT, g=KVH)
        v_lo = v_hid[:, 1, :].rearrange("p (t g e) -> p t g e", t=TT, g=KVH)
        q_hi = q_hid[:, 0, :].rearrange("p (s h t) -> p s h t", s=2, h=2)
        q_lo = q_hid[:, 1, :].rearrange("p (s h t) -> p s h t", s=2, h=2)
        hid_hi = v_hid[:, :, :].rearrange("p a (h t) -> p (a h) t", t=TOK)
        hid_lo = q_hid[:, :, :].rearrange("p a (h t) -> p (a h) t", t=TOK)
        p_raw_flat = p_raw[:, :, :].rearrange("p a t -> p (a t)")
        p_hi_flat = p_hi[:, :, :].rearrange("p a t -> p (a t)")
        p_lo_flat = p_lo[:, :, :].rearrange("p a t -> p (a t)")

        x_loaded = [sem(f"x_loaded{c}") for c in range(HALVES)]
        tables_loaded = sem("tables_loaded")
        decay_loaded = [sem(f"decay_loaded{i}") for i in range(4)]
        had_loaded = sem("had_loaded")
        w_loaded = [sem(f"w_loaded{s}") for s in range(2)]
        stored = sem("stored")
        w_hi_done, w_lo_done, had_done = sem("w_hi_done"), sem("w_lo_done"), sem("had_done")
        stats_done, mv_done, eps_done = sem("stats_done"), sem("mv_done"), sem("eps_done")
        half_set, rstd_done, xn_done = sem("half_set"), sem("rstd_done"), sem("xn_done")
        lin_full, lin_free = sem("lin_full"), sem("lin_free")
        x_hi_done, v_hi_done = sem("x_hi_done"), sem("v_hi_done")
        rope_sum, rope_hi, rope_lo = sem("rope_sum"), sem("rope_hi"), sem("rope_lo")
        s_full, mask_done, p_hi_done, p_lo_done = sem("s_full"), sem("mask_done"), sem("p_hi_done"), sem("p_lo_done")
        o_full, o_hi_done, o_lo_done = sem("o_full"), sem("o_hi_done"), sem("o_lo_done")
        y_full, x2_done = sem("y_full"), sem("x2_done")
        up_full, silu_done, hid_done = sem("up_full"), sem("silu_done"), sem("hid_done")
        hid_hi_done, hid_lo_done = sem("hid_hi_done"), sem("hid_lo_done")
        fly_done, w2_hi_done, w2_lo_done = sem("fly_done"), sem("w2_hi_done"), sem("w2_lo_done")
        t_full, t_hi_done, t_free = sem("t_full"), sem("t_hi_done"), sem("t_free")
        down_full, out_done = sem("down_full"), sem("out_done")

        block = ctx.enter_context(nc.Block())

        def rope_dst(item):
            kind, _, n = item
            if kind == "K":
                return k_hi[:, n % 2, :], k_lo[:, n % 2, :]
            return q_hi[:, n // 2 % 2, n % 2, :], q_lo[:, n // 2 % 2, n % 2, :]

        def w2_part(w, m):
            dc, n = divmod(m, 2)
            tiles = w[:, AT_W2:AT_W2 + HT * D].rearrange("p (a d) -> p a d", a=HT)
            return tiles[:, 4 * n:4 * n + 4, dc * P:(dc + 1) * P]

        @block.sync
        def _(sp):
            def load_chunk(n):
                if n >= 2:
                    sp.wait_ge(w_lo_done, n - 1)
                w, i, _ = CHUNKS[n]
                sp.dma_start(w_raw[:, n % 2, :], dram[w][i]).then_inc(w_loaded[n % 2], 16)

            def load_x(c):
                sp.dma_start(x_sb[:, c * TT:(c + 1) * TT, :], x[c]).then_inc(x_loaded[c], 16)

            def load_decay(i):
                sp.dma_start(decay_sb[:, 4 * i:4 * i + 4, :], decay[i]).then_inc(decay_loaded[i], 16)

            load_x(0)
            load_chunk(0)
            load_chunk(1)
            load_chunk(2)
            load_decay(0)
            load_chunk(3)
            load_chunk(4)
            load_decay(1)
            load_x(1)
            load_chunk(5)
            load_decay(2)
            load_decay(3)
            sp.dma_start(had_raw[:], hadamard).then_inc(had_loaded, 16)
            for n in range(6, len(CHUNKS)):
                load_chunk(n)
            for n in range(HALVES * TT):
                sp.wait_ge(out_done, n + 1)
                sp.dma_start(out[n], x_sb[:, n, :]).then_inc(stored, 16)
            sp.wait_ge(stored, 16 * HALVES * TT)

        @block.tensor
        def _(pe):
            def product(o, a_hi, a_lo, b_hi, b_lo, first, last, shared=False):
                pe.matmul(o, a_hi, b_hi, start=first, stop=False, skip_group_check=shared)
                pe.matmul(o, a_hi, b_lo, start=False, stop=False, skip_group_check=shared)
                return pe.matmul(o, a_lo, b_hi, start=False, stop=last, skip_group_check=shared)

            def lin_wait(item):
                n = LIN_NO[item]
                if n >= 2:
                    pe.wait_ge(lin_free, n - 1)
                return lin_bank[n % 2]

            def transpose_norm(dst, full, i, k):
                pe.wait_ge(xn_done, TT * (i + 1))
                for t in range(TT):
                    last = pe.transpose(dst[:, t * P:(t + 1) * P], xn[:, t, k * P:(k + 1) * P], ident_sb[:])
                last.then_inc(full, 1)

            def turn(i, k):
                transpose_norm(lin_wait(("X", i, k)), lin_full, i, k)

            def project(item):
                kind, c, h = item
                o = lin_wait(item)
                pe.wait_ge(lin_free, LIN_NO[("X", c, KD - 1)] + 1)
                chunk = ("wk", 0) if kind == "K" else ("wq", h // 4)
                pe.wait_ge(w_lo_done, CHUNK_NO[chunk] + 1)
                at = (AT_K if kind == "K" else AT_Q) + h * KD * P
                for k in range(KD):
                    a = slice(at + k * P, at + (k + 1) * P)
                    last = product(o[:], w_hi[:, a], w_lo[:, a], xt_hi[:, k, :], xt_lo[:, k, :],
                                   k == 0, k == KD - 1)
                last.then_inc(lin_full, 1)

            def project_values(c, t):
                o = lin_wait(("V", c, t))
                pe.wait_ge(lin_free, LIN_NO[("X", c, KD - 1)] + 1)
                pe.wait_ge(w_lo_done, CHUNK_NO[("wv", 0)] + 1)
                for k in range(KD):
                    a, b = slice(t * P, (t + 1) * P), slice(AT_V + k * 512, AT_V + (k + 1) * 512)
                    last = product(o[:], xt_hi[:, k, a], xt_lo[:, k, a], w_hi[:, b], w_lo[:, b],
                                   k == 0, k == KD - 1)
                last.then_inc(lin_full, 1)

            def scores(c, p):
                u, ks, qs = c * PAIRS + p, p // PPG % 2, p % 2
                pe.wait_ge(rope_lo, ROPE_NO[("Q", c, 2 * p + 1)] + 1)
                for s in (S_FIRST0, S_SECOND, S_FIRST1):
                    if u:
                        pe.wait_ge(mask_done, 3 * (u - 1) + s + 1)
                    if s == S_SECOND:
                        for b in range(BH):
                            a = slice(b * SEQ + P, (b + 1) * SEQ)
                            last = product(s_bank[s][:, b * 256:(b + 1) * 256], k_hi[:, ks, a], k_lo[:, ks, a],
                                           q_hi[:, qs, :, a], q_lo[:, qs, :, a], True, True)
                    else:
                        b = S_OF_SEQ.index(s)
                        a, i = slice(b * SEQ, b * SEQ + P), slice(b * SEQ, (b + 1) * SEQ)
                        last = product(s_bank[s][:], k_hi[:, ks, a], k_lo[:, ks, a],
                                       q_hi[:, qs, :, i], q_lo[:, qs, :, i], True, True)
                    last.then_inc(s_full, 1)

            def attend(c, p, b):
                u, g = c * PAIRS + p, p // PPG
                pe.wait_ge(p_lo_done, 3 * u + (S_SECOND, S_FIRST1)[b] + 1)
                pe.wait_ge(lin_free, LIN_NO[("V", c, TT - 1)] + 1)
                if 2 * u + b:
                    pe.wait_ge(o_lo_done, 2 * u + b)
                s = S_OF_SEQ[b]
                product(o_bank[:], v_hi[:, 2 * b, g, :], v_lo[:, 2 * b, g, :], p_hi[:, s, :], p_lo[:, s, :],
                        True, False)
                second = o_bank[:].rearrange("p (h t) -> p h t", h=2)[:, :, P:SEQ]
                a = slice(b * 256, (b + 1) * 256)
                product(second, v_hi[:, 2 * b + 1, g, :], v_lo[:, 2 * b + 1, g, :],
                        p_hi[:, S_SECOND, a], p_lo[:, S_SECOND, a], False, True).then_inc(o_full, 1)

            def project_out(c, p, b):
                u = c * PAIRS + p
                pe.wait_ge(o_lo_done, 2 * u + b + 1)
                pe.wait_ge(w_lo_done, CHUNK_NO[("wo", p // 2)] + 1)
                if c and p == 0:
                    pe.wait_ge(x2_done, BH * (c - 1) + b + 1)
                for h in range(2):
                    w = slice(AT_O + (2 * p + h) * D, AT_O + (2 * p + h + 1) * D)
                    for t in range(2):
                        a = slice(t * P, (t + 1) * P)
                        last = product(y_bank[b][:, t * D:(t + 1) * D], o_hi[:, b, h, a], o_lo[:, b, h, a],
                                       w_hi[:, w], w_lo[:, w], p == 0 and h == 0 and t == 0,
                                       p == PAIRS - 1 and h == 1 and t == 1, shared=True)
                if p == PAIRS - 1:
                    last.then_inc(y_full, 1)

            def up(c, h):
                n = c * HT + h
                pe.wait_ge(w_lo_done, CHUNK_NO[("w3", h // 4)] + 1)
                if n == 0:
                    pe.wait_ge(lin_free, len(LIN))
                if n == 1:
                    pe.wait_ge(mask_done, 3 * UNITS - 1)
                if n >= 2:
                    pe.wait_ge(hid_done, n - 1)
                if c and h == 0:
                    pe.wait_ge(t_free, W2_TILES + KD)
                for j in range(2):
                    at = AT_FF + (h // 4 * 2 + j) * CH + h % 4 * KD * P
                    for k in range(KD):
                        a = slice(at + k * P, at + (k + 1) * P)
                        last = product(up_bank[n % 2][j][:], w_hi[:, a], w_lo[:, a], xt_hi[:, k, :], xt_lo[:, k, :],
                                       k == 0, k == KD - 1)
                last.then_inc(up_full, 1)

            def transform(m):
                dc, n = divmod(m, 2)
                pe.wait_ge(w2_lo_done, dc + 1)
                if m == 0:
                    pe.wait_ge(had_done, 1)
                    pe.wait_ge(mask_done, 3 * UNITS)
                elif m == 1:
                    pe.wait_ge(o_lo_done, 2 * UNITS)
                else:
                    pe.wait_ge(t_free, m - 1)
                a = slice(n * 512, (n + 1) * 512)
                pe.matmul(t_bank[m % 2][:], had[:], p_hi_flat[:, a], start=True, stop=False)
                pe.matmul(t_bank[m % 2][:], had[:], p_lo_flat[:, a], start=False, stop=True).then_inc(t_full, 1)

            def down(c, t):
                n = c * TT + t
                pe.wait_ge(hid_lo_done, (c + 1) * HT)
                if c:
                    pe.wait_ge(out_done, n - TT + 1)
                elif t < 2:
                    pe.wait_ge(x2_done, HALVES * BH)
                    pe.wait_ge(t_free, W2_TILES)
                else:
                    pe.wait_ge(t_free, W2_TILES + KD)
                for h in range(HT):
                    a, w = slice(t * P, (t + 1) * P), slice(AT_W2 + h * D, AT_W2 + (h + 1) * D)
                    last = product(down_bank[t][:, 0:D], hid_hi[:, h, a], hid_lo[:, h, a], w_hi[:, w], w_lo[:, w],
                                   h == 0, h == HT - 1)
                last.then_inc(down_full, 1)

            pe.wait_ge(tables_loaded, 48)
            turn(0, 0)
            turn(0, 1)
            project(("K", 0, 0))
            for t in range(TT):
                project_values(0, t)
            project(("Q", 0, 0))
            project(("Q", 0, 1))
            for c in range(HALVES):
                for p in range(PAIRS):
                    last_pair = p == PAIRS - 1
                    scores(c, p)
                    if last_pair:
                        turn(c + 1, 0)
                        turn(c + 1, 1)
                    else:
                        project(("Q", c, 2 * p + 2))
                    if p:
                        project_out(c, p - 1, 1)
                    attend(c, p, 0)
                    if not last_pair:
                        project(("Q", c, 2 * p + 3))
                    elif c == 0:
                        project(("K", c + 1, 0))
                    else:
                        up(0, 0)
                    project_out(c, p, 0)
                    for item in step_rope(c, p)[2:]:
                        project(item)
                    attend(c, p, 1)
                if c == 0:
                    project_values(1, 0)
                    project_values(1, 1)
                    project_out(c, PAIRS - 1, 1)
                    project_values(1, 2)
                    project_values(1, 3)
                    project(("Q", 1, 0))
                    project(("Q", 1, 1))
                else:
                    up(0, 1)
                    project_out(c, PAIRS - 1, 1)
            for h in range(2, HT):
                up(0, h)
                if h in (5, 7):
                    transform(h - 5)
                    transform(h - 4)
            for k in range(KD):
                pe.wait_ge(t_free, W2_TILES - KD + k + 1)
                transpose_norm(t_bank[k], t_full, 3, k)
            for t in range(TT):
                down(0, t)
            for h in range(HT):
                up(1, h)
            for t in range(TT):
                down(1, t)

        @block.scalar
        def _(act):
            def high_weights(n):
                _, _, at = CHUNKS[n]
                act.wait_ge(w_loaded[n % 2], 16 * (n // 2 + 1))
                if n >= CHUNK_NO[("w1", 0)]:
                    i = (at - AT_Q) // CH
                    act.wait_ge(lin_full, LIN_NO[("Q", 1, 4 * i + 3)] + 1)
                act.activation(w_hi[:, at:at + CH], w_raw[:, n % 2, :], ACT.Copy).then_inc(w_hi_done, 1)

            def high_x(i):
                for k in range(KD):
                    n = LIN_NO[("X", i, k)]
                    act.wait_ge(lin_full, n + 1)
                    act.activation(xt_hi[:, k, :], lin_bank[n % 2][:], ACT.Copy).then_inc(x_hi_done, 1)

            def high_v(c, t):
                n = LIN_NO[("V", c, t)]
                act.wait_ge(lin_full, n + 1)
                act.activation(v_hi[:, t, :, :].rearrange("p g e -> p (g e)"), lin_bank[n % 2][:],
                               ACT.Copy).then_inc(v_hi_done, 1)

            def high_rope(item):
                r = ROPE_NO[item]
                act.wait_ge(rope_sum, r + 1)
                act.activation(rope_dst(item)[0], qk[:, r % 2, :], ACT.Copy).then_inc(rope_hi, 1)

            def high_p(u, s):
                n = 3 * u + s
                act.wait_ge(mask_done, n + 1)
                act.activation(p_hi[:, s, :], p_raw[:, n % 2, :], ACT.Copy).then_inc(p_hi_done, 1)

            def high_o(u, b):
                act.wait_ge(o_full, 2 * u + b + 1)
                act.activation(o_hi[:, b, :, :].rearrange("p h t -> p (h t)"), o_bank[:],
                               ACT.Copy).then_inc(o_hi_done, 1)

            def silu(n):
                act.wait_ge(up_full, n + 1)
                if n >= 2:
                    act.wait_ge(hid_done, n - 1)
                act.activation(rope_a[:, n % 2, :], up_bank[n % 2][0][:], ACT.Silu).then_inc(silu_done, 1)

            def high_hid(n):
                act.wait_ge(hid_done, n + 1)
                if n == 0:
                    act.wait_ge(o_full, 2 * UNITS)
                act.activation(hid_hi[:, n % HT, :], rope_b[:, n % 2, :], ACT.Copy).then_inc(hid_hi_done, 1)

            def high_w2(dc):
                act.wait_ge(fly_done, 3 * (dc + 1))
                if dc == 0:
                    act.wait_ge(o_full, 2 * UNITS)
                else:
                    act.wait_ge(t_full, 2 * dc)
                act.activation(p_hi_flat[:, 0:CH], p_raw_flat, ACT.Copy).then_inc(w2_hi_done, 1)

            def high_t(m):
                act.wait_ge(t_full, m + 1)
                if m < W2_TILES:
                    dst, src = w2_part(w_hi, m), t_bank[m % 2][:].rearrange("p (a d) -> p a d", a=4)
                else:
                    dst, src = xt_hi[:, m - W2_TILES, :], t_bank[m % 2][:]
                act.activation(dst, src, ACT.Copy).then_inc(t_hi_done, 1)

            act.dma_start(ident_sb[:], ident).then_inc(tables_loaded, 16)
            act.dma_start(cos_sb[:], cos).then_inc(tables_loaded, 16)
            act.dma_start(sin_sb[:], sin).then_inc(tables_loaded, 16)
            high_weights(0)
            high_weights(1)
            high_x(0)
            high_weights(2)
            high_rope(("K", 0, 0))
            for t in range(TT):
                high_v(0, t)
            high_weights(3)
            high_rope(("Q", 0, 0))
            high_rope(("Q", 0, 1))
            for c in range(HALVES):
                for p in range(PAIRS):
                    u = c * PAIRS + p
                    rope = step_rope(c, p)
                    for s in range(3):
                        high_p(u, s)
                    if p == PAIRS - 1:
                        high_x(c + 1)
                    if step_chunk(c, p) is not None:
                        high_weights(step_chunk(c, p))
                    for item in rope[:1]:
                        high_rope(item)
                    high_o(u, 0)
                    if p == PAIRS - 1:
                        if c == 0:
                            high_rope(("K", 1, 0))
                        else:
                            silu(0)
                    for item in rope[1:]:
                        high_rope(item)
                    high_o(u, 1)
                if c == 0:
                    for t in range(TT):
                        high_v(1, t)
                    high_rope(("Q", 1, 0))
                    high_rope(("Q", 1, 1))
            act.wait_ge(had_loaded, 16)
            act.activation(had[:], had_raw[:], ACT.Copy).then_inc(had_done, 1)
            high_hid(0)
            for n in range(1, HALVES * HT):
                silu(n)
                high_hid(n)
                if n == 3:
                    high_w2(0)
                if n == 5:
                    high_t(0)
                    high_t(1)
                    high_w2(1)
                if n == 7:
                    for m in range(2, W2_TILES + KD):
                        high_t(m)

        @block.gpsimd
        def _(pool):
            def inverse_deviation(i):
                pool.wait_ge(eps_done, i + 1)
                pool.tensor_tensor(rstd[:], var_eps[:], minus_half[:], ALU.pow).then_inc(rstd_done, 1)

            def rope_add(item):
                r = ROPE_NO[item]
                pool.wait_ge(lin_free, LIN_NO[item] + 1)
                if r >= 2:
                    pool.wait_ge(rope_hi, r - 1)
                pool.tensor_tensor(qk[:, r % 2, :], rope_a[:, r % 2, :], rope_b[:, r % 2, :],
                                   ALU.add).then_inc(rope_sum, 1)

            def low_rope(item):
                r = ROPE_NO[item]
                hi, lo = rope_dst(item)
                pool.wait_ge(rope_hi, r + 1)
                pool.tensor_tensor(lo, qk[:, r % 2, :], hi.bitcast(F32), ALU.subtract).then_inc(rope_lo, 1)

            def low_p(u, s):
                n = 3 * u + s
                pool.wait_ge(p_hi_done, n + 1)
                pool.tensor_tensor(p_lo[:, s, :], p_raw[:, n % 2, :], p_hi[:, s, :].bitcast(F32),
                                   ALU.subtract).then_inc(p_lo_done, 1)

            def low_hid(n):
                pool.wait_ge(hid_hi_done, n + 1)
                pool.tensor_tensor(hid_lo[:, n % HT, :], rope_b[:, n % 2, :], hid_hi[:, n % HT, :].bitcast(F32),
                                   ALU.subtract).then_inc(hid_lo_done, 1)

            pool.memset(minus_half[:], -0.5).then_inc(half_set, 1)
            pool.wait_ge(half_set, 1)
            inverse_deviation(0)
            for item in (("K", 0, 0), ("Q", 0, 0), ("Q", 0, 1)):
                rope_add(item)
                low_rope(item)
            for c in range(HALVES):
                for p in range(PAIRS):
                    for s in range(3):
                        low_p(c * PAIRS + p, s)
                    for item in step_rope(c, p):
                        rope_add(item)
                        low_rope(item)
                    if p == 5:
                        inverse_deviation(c + 1)
                if c == 0:
                    for item in (("K", 1, 0), ("Q", 1, 0), ("Q", 1, 1)):
                        rope_add(item)
                        low_rope(item)
            for n in range(HALVES * HT):
                low_hid(n)
                if n == 2:
                    inverse_deviation(3)

        @block.vector
        def _(dve):
            def norm_stats(i):
                half = i % HALVES
                if i < HALVES:
                    dve.wait_ge(x_loaded[half], 16)
                else:
                    dve.wait_ge(x2_done, BH * (half + 1))
                for t in range(TT):
                    dve.bn_stats(stats[:, t, :], x_sb[:, half * TT + t, :]).then_inc(stats_done, 1)
                for t in range(TT):
                    dve.wait_ge(stats_done, TT * i + t + 1)
                    dve.bn_aggr(mean_var[:, t, :], stats[:, t, :]).then_inc(mv_done, 1)
                dve.wait_ge(mv_done, TT * (i + 1))
                dve.tensor_scalar(var_eps[:], mean_var[:, :, 1], EPS, None, ALU.add).then_inc(eps_done, 1)

            def norm_apply(i):
                half = i % HALVES
                dve.wait_ge(rstd_done, i + 1)
                if i:
                    dve.wait_ge(lin_full, LIN_NO[("X", i - 1, KD - 1)] + 1)
                for t in range(TT):
                    dve.tensor_scalar(xn[:, t, :], x_sb[:, half * TT + t, :], mean_var[:, t, 0:1], rstd[:, t:t + 1],
                                      ALU.subtract, ALU.mult).then_inc(xn_done, 1)

            def low_weights(n):
                _, _, at = CHUNKS[n]
                dve.wait_ge(w_hi_done, n + 1)
                dve.tensor_tensor(w_lo[:, at:at + CH], w_raw[:, n % 2, :], w_hi[:, at:at + CH].bitcast(F32),
                                  ALU.subtract).then_inc(w_lo_done, 1)

            def low_x(i):
                for k in range(KD):
                    n = LIN_NO[("X", i, k)]
                    dve.wait_ge(x_hi_done, X_NO[("X", i, k)] + 1)
                    dve.tensor_tensor(xt_lo[:, k, :], lin_bank[n % 2][:], xt_hi[:, k, :].bitcast(F32),
                                      ALU.subtract).then_inc(lin_free, 1)

            def low_v(c, t):
                n = LIN_NO[("V", c, t)]
                dve.wait_ge(v_hi_done, V_NO[("V", c, t)] + 1)
                dve.tensor_tensor(v_lo[:, t, :, :].rearrange("p g e -> p (g e)"), lin_bank[n % 2][:],
                                  v_hi[:, t, :, :].rearrange("p g e -> p (g e)").bitcast(F32),
                                  ALU.subtract).then_inc(lin_free, 1)

            def rotate(item):
                n, r = LIN_NO[item], ROPE_NO[item]
                dve.wait_ge(lin_full, n + 1)
                if r >= 2:
                    dve.wait_ge(rope_sum, r - 1)
                src = lin_bank[n % 2][:].rearrange("p (b t) -> p b t", b=BH)
                a = rope_a[:, r % 2, :].rearrange("p (b t) -> p b t", b=BH)
                b = rope_b[:, r % 2, :].rearrange("p (b t) -> p b t", b=BH)
                table = [tb[:].unsqueeze(1).broadcast_to([P, BH, SEQ]) for tb in (cos_sb, sin_sb)]
                dve.tensor_tensor(a, src, table[0], ALU.mult)
                h = P // 2
                dve.tensor_tensor(b[0:h], src[h:P], table[1][h:P], ALU.mult)
                dve.tensor_tensor(b[h:P], src[0:h], table[1][0:h], ALU.mult).then_inc(lin_free, 1)

            def mask(c, p, s):
                n = 3 * (c * PAIRS + p) + s
                dve.wait_ge(s_full, n + 1)
                if c == 0 and p % 2 == 0:
                    dve.wait_ge(decay_loaded[p // 2], 16)
                if n >= 2:
                    dve.wait_ge(p_lo_done, n - 1)
                table = decay_sb[:, 2 * p:2 * p + 2, :]
                if s == S_SECOND:
                    table = table[:, :, 0:P].unsqueeze(1).broadcast_to([P, BH, 2, P])
                    src = s_bank[s][:].rearrange("p (b h t) -> p b h t", b=BH, h=2)
                    dst = p_raw[:, n % 2, :].rearrange("p (b h t) -> p b h t", b=BH, h=2)
                else:
                    src = s_bank[s][:].rearrange("p (h t) -> p h t", h=2)
                    dst = p_raw[:, n % 2, :].rearrange("p (h t) -> p h t", h=2)
                dve.tensor_tensor(dst, src, table, ALU.mult).then_inc(mask_done, 1)

            def low_o(u, b):
                dve.wait_ge(o_hi_done, 2 * u + b + 1)
                dve.tensor_tensor(o_lo[:, b, :, :].rearrange("p h t -> p (h t)"), o_bank[:],
                                  o_hi[:, b, :, :].rearrange("p h t -> p (h t)").bitcast(F32),
                                  ALU.subtract).then_inc(o_lo_done, 1)

            def add_attention(c):
                for b in range(BH):
                    dve.wait_ge(y_full, BH * c + b + 1)
                    tiles = x_sb[:, c * TT + 2 * b:c * TT + 2 * b + 2, :]
                    dve.tensor_tensor(tiles, y_bank[b][:].rearrange("p (t d) -> p t d", t=2), tiles,
                                      ALU.add).then_inc(x2_done, 1)

            def hidden(n):
                dve.wait_ge(silu_done, n + 1)
                if n >= 2:
                    dve.wait_ge(hid_lo_done, n - 1)
                dve.tensor_tensor(rope_b[:, n % 2, :], up_bank[n % 2][1][:], rope_a[:, n % 2, :],
                                  ALU.mult).then_inc(hid_done, 1)

            def butterfly(dc, step):
                slot = CHUNK_NO[("w2", dc)] % 2
                if step == 0:
                    dve.wait_ge(w_loaded[slot], 16 * (CHUNK_NO[("w2", dc)] // 2 + 1))
                    if dc == 0:
                        dve.wait_ge(p_lo_done, 3 * UNITS)
                    else:
                        dve.wait_ge(w2_lo_done, dc)
                else:
                    dve.wait_ge(fly_done, 3 * dc + step)
                src, dst = w_raw[:, slot, :], p_raw_flat
                if step == 1:
                    src, dst = dst, src
                m = 1 << step
                s = src.rearrange("p (m two r) -> p m two r", m=m, two=2)
                d = dst.rearrange("p (m two r) -> p m two r", m=m, two=2)
                dve.tensor_tensor(d[:, :, 0, :], s[:, :, 0, :], s[:, :, 1, :], ALU.add)
                dve.tensor_tensor(d[:, :, 1, :], s[:, :, 0, :], s[:, :, 1, :], ALU.subtract).then_inc(fly_done, 1)

            def low_w2(dc):
                dve.wait_ge(w2_hi_done, dc + 1)
                dve.tensor_tensor(p_lo_flat[:, 0:CH], p_raw_flat, p_hi_flat[:, 0:CH].bitcast(F32),
                                  ALU.subtract).then_inc(w2_lo_done, 1)

            def low_t(m):
                dve.wait_ge(t_hi_done, m + 1)
                if m < W2_TILES:
                    dst, src = w2_part(w_lo, m), t_bank[m % 2][:].rearrange("p (a d) -> p a d", a=4)
                    hi = w2_part(w_hi, m)
                else:
                    k = m - W2_TILES
                    dst, src, hi = xt_lo[:, k, :], t_bank[m % 2][:], xt_hi[:, k, :]
                dve.tensor_tensor(dst, src, hi.bitcast(F32), ALU.subtract).then_inc(t_free, 1)

            def finish(n):
                dve.wait_ge(down_full, n + 1)
                dve.tensor_tensor(x_sb[:, n, :], down_bank[n % TT][:, 0:D], x_sb[:, n, :],
                                  ALU.add).then_inc(out_done, 1)

            norm_stats(0)
            low_weights(0)
            norm_apply(0)
            low_weights(1)
            low_x(0)
            dve.wait_ge(tables_loaded, 48)
            rotate(("K", 0, 0))
            low_weights(2)
            for t in range(TT):
                low_v(0, t)
            rotate(("Q", 0, 0))
            low_weights(3)
            rotate(("Q", 0, 1))
            for c in range(HALVES):
                for p in range(PAIRS):
                    u = c * PAIRS + p
                    rope = step_rope(c, p)
                    for s in range(3):
                        mask(c, p, s)
                    if p == PAIRS - 1:
                        low_x(c + 1)
                    for item in rope[:1]:
                        rotate(item)
                    if step_chunk(c, p) is not None:
                        low_weights(step_chunk(c, p))
                    low_o(u, 0)
                    if p == PAIRS - 1:
                        if c == 0:
                            rotate(("K", 1, 0))
                        else:
                            hidden(0)
                    for item in rope[1:]:
                        rotate(item)
                    low_o(u, 1)
                    if p == 5:
                        norm_stats(c + 1)
                    if p == 6:
                        norm_apply(c + 1)
                if c == 0:
                    for t in range(TT):
                        low_v(1, t)
                    rotate(("Q", 1, 0))
                    add_attention(0)
                    rotate(("Q", 1, 1))
            hidden(1)
            add_attention(1)
            hidden(2)
            norm_stats(3)
            hidden(3)
            butterfly(0, 0)
            butterfly(0, 1)
            butterfly(0, 2)
            low_w2(0)
            hidden(4)
            norm_apply(3)
            butterfly(1, 0)
            hidden(5)
            butterfly(1, 1)
            butterfly(1, 2)
            low_t(0)
            low_t(1)
            low_w2(1)
            hidden(6)
            hidden(7)
            for m in range(2, W2_TILES + KD):
                low_t(m)
            for n in range(TT):
                finish(n)
            for n in range(HT, 2 * HT):
                hidden(n)
            for n in range(TT, 2 * TT):
                finish(n)


def tables():
    f = np.float32
    inv_freq = f(1.0) / f(10000.0) ** (np.arange(0, P, 2, dtype=f) / f(P))
    angle = (np.arange(SEQ, dtype=f)[None, :] * inv_freq[:, None]).astype(f).astype(np.float64)
    cos = np.concatenate([np.cos(angle)] * 2).astype(f)
    sin = np.concatenate([np.sin(angle), -np.sin(angle)]).astype(f)
    lam = np.exp2(f(-8.0) * np.arange(1, HEADS + 1, dtype=f) / f(HEADS)).astype(np.float64)
    lag = np.arange(SEQ)[None, :] - np.arange(P)[:, None]
    decay = np.where(lag[:, None, :] >= 0, np.exp(-lam[None, :, None] * np.maximum(lag, 0)[:, None, :]), 0.0)
    decay = decay.astype(f).reshape(P, 4, 4, SEQ).transpose(1, 0, 2, 3)
    signs = np.array([[-1.0 if bin(i & j).count("1") % 2 else 1.0 for j in range(P)] for i in range(P)])
    return {"cos": cos, "sin": sin, "decay": decay, "ident": np.eye(P, dtype=f),
            "hadamard": (signs / np.sqrt(HID)).astype(f)}


def layouts(x, wq, wk, wv, wo, w1, w2, w3):
    def stationary(w):
        r = w.reshape(-1, 4, P, KD, P).transpose(0, 4, 1, 3, 2)
        return r.reshape(-1, P, 4 * KD * P)
    return {
        "x": x.reshape(HALVES, TT, P, D).transpose(0, 2, 1, 3),
        "wk": stationary(wk),
        "wv": wv.reshape(1, KVH * P, KD, P).transpose(0, 3, 2, 1).reshape(1, P, CH),
        "wq": stationary(wq),
        "wo": wo.reshape(D, 4, 4, P).transpose(1, 3, 2, 0).reshape(4, P, CH),
        "w1": stationary(w1),
        "w3": stationary(w3),
        "w2": w2.reshape(2, P, HT, P).transpose(0, 3, 2, 1).reshape(2, P, CH),
    }


def kernel(L0_attn_x, L0_attn_wq, L0_attn_wk, L0_attn_wv, L0_attn_wo, L0_ffn_W1, L0_ffn_W2, L0_ffn_W3):
    import concourse.bacc as bacc
    from concourse.bass_utils import run_bass_kernel_spmd

    laid = layouts(*(np.asarray(a) for a in (L0_attn_x, L0_attn_wq, L0_attn_wk, L0_attn_wv, L0_attn_wo,
                                              L0_ffn_W1, L0_ffn_W2, L0_ffn_W3)))
    laid.update(tables())
    nc = bacc.Bacc("TRN2", target_bir_lowering=False, num_devices=1)
    arrays, args = {}, {}
    for name, a in laid.items():
        a = np.ascontiguousarray(a)
        arrays[f"in_{name}"] = a
        args[name] = nc.dram_tensor(f"in_{name}", a.shape, mybir.dt.from_np(a.dtype), kind="ExternalInput").ap()
    out = nc.dram_tensor("out", (HALVES * TT, P, D), F32, kind="ExternalOutput").ap()
    build(nc, out=out, **args)
    r = run_bass_kernel_spmd(nc, [arrays], core_ids=[0])
    return r.results[0]["out"].reshape(NSEQ, SEQ, D)
```

```python
from contextlib import ExitStack

import numpy as np

import concourse.bass as bass
from concourse import mybir

F32 = mybir.dt.float32
F32R = mybir.dt.float32r
ALU = mybir.AluOpType
ACT = mybir.ActivationFunctionType

P = 128
D = 256
KD = D // P
SEQ = 256
NSEQ = 4
HALVES = 2
TOK = NSEQ * SEQ // HALVES
BH = TOK // SEQ
TT = TOK // P
HEADS = 16
KVH = 4
PAIRS = HEADS // 2
PPG = PAIRS // KVH
HID = 1024
HT = HID // P
EPS = 1e-5
UNITS = HALVES * PAIRS

CH = 1024
AT_K, AT_V, AT_Q, AT_O = 0, CH, 2 * CH, 6 * CH
W_COLS = 10 * CH
AT_W2 = AT_K
AT_FF = AT_Q
CHUNKS = [("wk", 0, AT_K), ("wq", 0, AT_Q), ("wv", 0, AT_V), ("wq", 1, AT_Q + CH), ("wo", 0, AT_O),
          ("wq", 2, AT_Q + 2 * CH), ("wo", 1, AT_O + CH), ("wq", 3, AT_Q + 3 * CH), ("wo", 2, AT_O + 2 * CH),
          ("wo", 3, AT_O + 3 * CH),
          ("w1", 0, AT_FF), ("w3", 0, AT_FF + CH), ("w1", 1, AT_FF + 2 * CH), ("w3", 1, AT_FF + 3 * CH),
          ("w2", 0, AT_W2), ("w2", 1, AT_W2 + CH)]
CHUNK_NO = {(w, i): n for n, (w, i, _) in enumerate(CHUNKS)}
FIRST_CHUNKS = 4

START = ([("X", 0, k) for k in range(KD)] + [("K", 0, 0), ("Q", 0, 0), ("Q", 0, 1)]
         + [("V", 0, t) for t in range(TT)])


def fills(c, p):
    if p < PAIRS - 2:
        a, b = ("Q", c, 2 * p + 4), ("Q", c, 2 * p + 5)
        last = [("K", c, p // PPG + 1)] if p % PPG == 0 else []
        if p == PAIRS - 3:
            last = [("X", c + 1, k) for k in range(KD)]
        if p:
            return [a], [], [b], last
        if c == 0:
            return [("Q", 0, 2), ("Q", 0, 3)], [], [a, b], last
        return [a], [("V", 1, 0), ("V", 1, 1)], [b, ("V", 1, 2), ("V", 1, 3)], last
    if c:
        return [], [], [], []
    return ([("K", 1, 0)], [], [("Q", 1, 0)], [("Q", 1, 1)]) if p == PAIRS - 2 else ([("Q", 1, 2)], [], [("Q", 1, 3)], [])


def unit_chunk(c, p):
    if c == 0:
        return FIRST_CHUNKS + p if FIRST_CHUNKS + p < CHUNK_NO[("w1", 0)] else None
    return CHUNK_NO[("w1", 0)] + p // 2 if p % 2 == 0 else None


LIN = START + [i for c in range(HALVES) for p in range(PAIRS) for f in fills(c, p) for i in f]
LIN_NO = {item: n for n, item in enumerate(LIN)}
ROPE = [i for i in LIN if i[0] in "KQ"]
ROPE_NO = {item: n for n, item in enumerate(ROPE)}
V_NO = {item: n for n, item in enumerate(i for i in LIN if i[0] == "V")}
X_NO = {item: n for n, item in enumerate(i for i in LIN if i[0] == "X")}
FIRST_ROPE = 3

S_FIRST0, S_SECOND, S_FIRST1 = range(3)
S_OF_SEQ = (S_FIRST0, S_FIRST1)
W2_TILES = 4


def build(nc, x, wk, wv, wq, wo, w1, w3, w2, cos, sin, decay, ident, hadamard, out):
    dram = {"wk": wk, "wv": wv, "wq": wq, "wo": wo, "w1": w1, "w3": w3, "w2": w2}

    with ExitStack() as ctx:
        def sb(name, shape, dt=F32):
            return ctx.enter_context(nc.sbuf_tensor(name, shape, dt))

        def sem(name):
            return ctx.enter_context(nc.semaphore(name))

        w_hi = sb("w_hi", [P, W_COLS], F32R)
        w_lo = sb("w_lo", [P, W_COLS], F32R)
        w_raw = sb("w_raw", [P, 2, CH])
        x_sb = sb("x_sb", [P, HALVES * TT, D])
        xn = sb("xn", [P, TT, D])
        xt_hi = sb("xt_hi", [P, KD, TOK], F32R)
        xt_lo = sb("xt_lo", [P, KD, TOK], F32R)
        k_hi = sb("k_hi", [P, 2, TOK], F32R)
        k_lo = sb("k_lo", [P, 2, TOK], F32R)
        v_hid = sb("v_hid", [P, 2, TT * KVH * P], F32R)
        q_hid = sb("q_hid", [P, 2, 2 * 2 * TOK], F32R)
        rope_a = sb("rope_a", [P, 2, TOK])
        rope_b = sb("rope_b", [P, 2, TOK])
        qk = sb("qk", [P, 2, TOK])
        p_raw = sb("p_raw", [P, 2, TOK])
        p_hi = sb("p_hi", [P, 3, TOK], F32R)
        p_lo = sb("p_lo", [P, 3, TOK], F32R)
        o_hi = sb("o_hi", [P, BH, 2, SEQ], F32R)
        o_lo = sb("o_lo", [P, BH, 2, SEQ], F32R)
        cos_sb = sb("cos_sb", [P, SEQ])
        sin_sb = sb("sin_sb", [P, SEQ])
        decay_sb = sb("decay_sb", [P, HEADS, SEQ])
        ident_sb = sb("ident_sb", [P, P])
        had_raw = sb("had_raw", [P, P])
        had = sb("had", [P, P], F32R)
        stats = sb("stats", [P, TT, 6])
        mean_var = sb("mean_var", [P, TT, 2])
        var_eps = sb("var_eps", [P, TT])
        rstd = sb("rstd", [P, TT])
        minus_half = sb("minus_half", [P, TT])

        bank = [ctx.enter_context(nc.psum_tensor(f"bank{i}", [P, 512], F32)) for i in range(8)]
        lin_bank = bank[0:2]
        s_bank = bank[2:5]
        o_bank = bank[5]
        y_bank = bank[6:8]
        up_bank = (bank[0:2], bank[2:4])
        t_bank = bank[4:6]
        down_bank = (bank[6], bank[7], bank[4], bank[5])

        v_hi = v_hid[:, 0, :].rearrange("p (t g e) -> p t g e", t=TT, g=KVH)
        v_lo = v_hid[:, 1, :].rearrange("p (t g e) -> p t g e", t=TT, g=KVH)
        q_hi = q_hid[:, 0, :].rearrange("p (s h t) -> p s h t", s=2, h=2)
        q_lo = q_hid[:, 1, :].rearrange("p (s h t) -> p s h t", s=2, h=2)
        hid_hi = v_hid[:, :, :].rearrange("p a (h t) -> p (a h) t", t=TOK)
        hid_lo = q_hid[:, :, :].rearrange("p a (h t) -> p (a h) t", t=TOK)
        xn_flat = xn[:, :, :].rearrange("p t d -> p (t d)")

        x_loaded = [sem(f"x_loaded{c}") for c in range(HALVES)]
        tables_loaded = sem("tables_loaded")
        decay_loaded = [sem(f"decay_loaded{i}") for i in range(4)]
        had_loaded = sem("had_loaded")
        w_loaded = [sem(f"w_loaded{s}") for s in range(2)]
        stored = sem("stored")
        w_hi_done, w_lo_done, had_done = sem("w_hi_done"), sem("w_lo_done"), sem("had_done")
        stats_done, mv_done, eps_done = sem("stats_done"), sem("mv_done"), sem("eps_done")
        half_set, rstd_done, xn_done = sem("half_set"), sem("rstd_done"), sem("xn_done")
        lin_full, lin_free = sem("lin_full"), sem("lin_free")
        x_hi_done, v_hi_done = sem("x_hi_done"), sem("v_hi_done")
        swapped, rope_parts, rope_sum = sem("swapped"), sem("rope_parts"), sem("rope_sum")
        rope_hi, rope_lo = sem("rope_hi"), sem("rope_lo")
        s_full, mask_done, p_hi_done = sem("s_full"), sem("mask_done"), sem("p_hi_done")
        p_lo_dve, p_lo_pool = sem("p_lo_dve"), sem("p_lo_pool")
        o_full, o_hi_done, o_lo_done = sem("o_full"), sem("o_hi_done"), sem("o_lo_done")
        y_full, x2_done = sem("y_full"), sem("x2_done")
        up_full, silu_done, hid_done = sem("up_full"), sem("silu_done"), sem("hid_done")
        hid_hi_done, hid_lo_done = sem("hid_hi_done"), sem("hid_lo_done")
        fly_done, w2_hi_done, w2_lo_done = sem("fly_done"), sem("w2_hi_done"), sem("w2_lo_done")
        t_full, t_hi_done, t_free = sem("t_full"), sem("t_hi_done"), sem("t_free")
        down_full, out_done = sem("down_full"), sem("out_done")

        block = ctx.enter_context(nc.Block())

        def rope_dst(item):
            kind, _, n = item
            if kind == "K":
                return k_hi[:, n % 2, :], k_lo[:, n % 2, :]
            return q_hi[:, n // 2 % 2, n % 2, :], q_lo[:, n // 2 % 2, n % 2, :]

        def w2_part(w, m):
            return w[:, AT_W2 + m * 512:AT_W2 + (m + 1) * 512]

        def w2_tile(w, h):
            return w[:, AT_W2:AT_W2 + 2 * CH].rearrange("p (c a d) -> p c a d", c=2, a=HT)[:, :, h, :]

        @block.sync
        def _(sp):
            def load_chunk(n):
                if n >= 2:
                    sp.wait_ge(w_lo_done, n - 1)
                w, i, _ = CHUNKS[n]
                sp.dma_start(w_raw[:, n % 2, :], dram[w][i]).then_inc(w_loaded[n % 2], 16)

            def load_x(c):
                sp.dma_start(x_sb[:, c * TT:(c + 1) * TT, :], x[c]).then_inc(x_loaded[c], 16)

            def load_decay(i):
                sp.dma_start(decay_sb[:, 4 * i:4 * i + 4, :], decay[i]).then_inc(decay_loaded[i], 16)

            load_x(0)
            for n in range(3):
                load_chunk(n)
            load_decay(0)
            load_chunk(3)
            load_chunk(4)
            load_decay(1)
            load_x(1)
            load_chunk(5)
            load_decay(2)
            load_decay(3)
            sp.dma_start(had_raw[:], hadamard).then_inc(had_loaded, 16)
            for n in range(6, len(CHUNKS)):
                load_chunk(n)
            for n in range(HALVES * TT):
                sp.wait_ge(out_done, n + 1)
                sp.dma_start(out[n], x_sb[:, n, :]).then_inc(stored, 16)
            sp.wait_ge(stored, 16 * HALVES * TT)

        @block.tensor
        def _(pe):
            def product(o, a_hi, a_lo, b_hi, b_lo, first, last, shared=False):
                pe.matmul(o, a_hi, b_hi, start=first, stop=False, skip_group_check=shared)
                pe.matmul(o, a_hi, b_lo, start=False, stop=False, skip_group_check=shared)
                return pe.matmul(o, a_lo, b_hi, start=False, stop=last, skip_group_check=shared)

            def lin_wait(item):
                n = LIN_NO[item]
                if n >= 2:
                    pe.wait_ge(lin_free, n - 1)
                return lin_bank[n % 2]

            def transpose_norm(dst, full, i, k):
                pe.wait_ge(xn_done, TT * (i + 1))
                for t in range(TT):
                    last = pe.transpose(dst[:, t * P:(t + 1) * P], xn[:, t, k * P:(k + 1) * P], ident_sb[:])
                last.then_inc(full, 1)

            def turn(i, k):
                transpose_norm(lin_wait(("X", i, k)), lin_full, i, k)

            def project(item):
                kind, c, h = item
                o = lin_wait(item)
                pe.wait_ge(lin_free, LIN_NO[("X", c, KD - 1)] + 1)
                chunk = ("wk", 0) if kind == "K" else ("wq", h // 4)
                pe.wait_ge(w_lo_done, CHUNK_NO[chunk] + 1)
                at = (AT_K if kind == "K" else AT_Q) + h * KD * P
                for k in range(KD):
                    a = slice(at + k * P, at + (k + 1) * P)
                    last = product(o[:], w_hi[:, a], w_lo[:, a], xt_hi[:, k, :], xt_lo[:, k, :],
                                   k == 0, k == KD - 1)
                last.then_inc(lin_full, 1)

            def project_values(c, t):
                o = lin_wait(("V", c, t))
                pe.wait_ge(lin_free, LIN_NO[("X", c, KD - 1)] + 1)
                pe.wait_ge(w_lo_done, CHUNK_NO[("wv", 0)] + 1)
                for k in range(KD):
                    a, b = slice(t * P, (t + 1) * P), slice(AT_V + k * 512, AT_V + (k + 1) * 512)
                    last = product(o[:], xt_hi[:, k, a], xt_lo[:, k, a], w_hi[:, b], w_lo[:, b],
                                   k == 0, k == KD - 1)
                last.then_inc(lin_full, 1)

            def scores(c, p):
                u, ks, qs = c * PAIRS + p, p // PPG % 2, p % 2
                needed = max(ROPE_NO[("Q", c, 2 * p + 1)], ROPE_NO[("K", c, p // PPG)])
                pe.wait_ge(rope_lo, needed + 1)
                for s in (S_FIRST0, S_SECOND, S_FIRST1):
                    if u:
                        pe.wait_ge(mask_done, 3 * (u - 1) + s + 1)
                    if s == S_SECOND:
                        for b in range(BH):
                            a = slice(b * SEQ + P, (b + 1) * SEQ)
                            last = product(s_bank[s][:, b * 256:(b + 1) * 256], k_hi[:, ks, a], k_lo[:, ks, a],
                                           q_hi[:, qs, :, a], q_lo[:, qs, :, a], True, True)
                    else:
                        b = S_OF_SEQ.index(s)
                        a, i = slice(b * SEQ, b * SEQ + P), slice(b * SEQ, (b + 1) * SEQ)
                        last = product(s_bank[s][:], k_hi[:, ks, a], k_lo[:, ks, a],
                                       q_hi[:, qs, :, i], q_lo[:, qs, :, i], True, True)
                    last.then_inc(s_full, 1)

            def attend(c, p, b):
                u, g = c * PAIRS + p, p // PPG
                if b == 0:
                    pe.wait_ge(p_lo_dve, 2 * (u + 1))
                else:
                    pe.wait_ge(p_lo_pool, u + 1)
                pe.wait_ge(lin_free, LIN_NO[("V", c, 2 * b + 1)] + 1)
                if 2 * u + b:
                    pe.wait_ge(o_lo_done, 2 * u + b)
                s = S_OF_SEQ[b]
                product(o_bank[:], v_hi[:, 2 * b, g, :], v_lo[:, 2 * b, g, :], p_hi[:, s, :], p_lo[:, s, :],
                        True, False)
                second = o_bank[:].rearrange("p (h t) -> p h t", h=2)[:, :, P:SEQ]
                a = slice(b * 256, (b + 1) * 256)
                product(second, v_hi[:, 2 * b + 1, g, :], v_lo[:, 2 * b + 1, g, :],
                        p_hi[:, S_SECOND, a], p_lo[:, S_SECOND, a], False, True).then_inc(o_full, 1)

            def project_out(c, p, b):
                u = c * PAIRS + p
                pe.wait_ge(o_lo_done, 2 * u + b + 1)
                pe.wait_ge(w_lo_done, CHUNK_NO[("wo", p // 2)] + 1)
                if c and p == 0:
                    pe.wait_ge(x2_done, BH * (c - 1) + b + 1)
                for h in range(2):
                    w = slice(AT_O + (2 * p + h) * D, AT_O + (2 * p + h + 1) * D)
                    for t in range(2):
                        a = slice(t * P, (t + 1) * P)
                        last = product(y_bank[b][:, t * D:(t + 1) * D], o_hi[:, b, h, a], o_lo[:, b, h, a],
                                       w_hi[:, w], w_lo[:, w], p == 0 and h == 0 and t == 0,
                                       p == PAIRS - 1 and h == 1 and t == 1, shared=True)
                if p == PAIRS - 1:
                    last.then_inc(y_full, 1)

            def up(c, h):
                n = c * HT + h
                pe.wait_ge(w_lo_done, CHUNK_NO[("w3", h // 4)] + 1)
                if n == 0:
                    pe.wait_ge(lin_free, len(LIN))
                if n == 1:
                    pe.wait_ge(mask_done, 3 * UNITS - 1)
                if n >= 2:
                    pe.wait_ge(hid_done, n - 1)
                if c and h == 0:
                    pe.wait_ge(t_free, W2_TILES + KD)
                for j in range(2):
                    at = AT_FF + (h // 4 * 2 + j) * CH + h % 4 * KD * P
                    for k in range(KD):
                        a = slice(at + k * P, at + (k + 1) * P)
                        last = product(up_bank[n % 2][j][:], w_hi[:, a], w_lo[:, a], xt_hi[:, k, :], xt_lo[:, k, :],
                                       k == 0, k == KD - 1)
                last.then_inc(up_full, 1)

            def transform(m):
                pe.wait_ge(w2_lo_done, m // 2 + 1)
                if m == 0:
                    pe.wait_ge(had_done, 1)
                    pe.wait_ge(mask_done, 3 * UNITS)
                elif m == 1:
                    pe.wait_ge(o_lo_done, 2 * UNITS)
                else:
                    pe.wait_ge(t_free, m - 1)
                pe.matmul(t_bank[m % 2][:], had[:], w2_part(w_hi, m), start=True, stop=False)
                pe.matmul(t_bank[m % 2][:], had[:], w2_part(w_lo, m), start=False, stop=True).then_inc(t_full, 1)

            def down(c, h, tiles):
                pe.wait_ge(hid_lo_done, c * HT + h + 1)
                for t in tiles:
                    if h == 0 and c:
                        pe.wait_ge(out_done, t + 1)
                    elif h == 0 and t == 0:
                        pe.wait_ge(x2_done, HALVES * BH)
                        pe.wait_ge(t_free, W2_TILES)
                    elif h == 0 and t == 2:
                        pe.wait_ge(t_free, W2_TILES + KD)
                    a = slice(t * P, (t + 1) * P)
                    last = product(down_bank[t][:, 0:D], hid_hi[:, h, a], hid_lo[:, h, a],
                                   w2_tile(w_hi, h), w2_tile(w_lo, h), h == 0, h == HT - 1)
                    if h == HT - 1:
                        last.then_inc(down_full, 1)

            def fill(items):
                for item in items:
                    if item[0] == "X":
                        turn(*item[1:])
                    elif item[0] == "V":
                        project_values(*item[1:])
                    else:
                        project(item)

            pe.wait_ge(tables_loaded, 48)
            fill(START)
            for u in range(UNITS):
                c, p = divmod(u, PAIRS)
                after_scores, before_first, between, before_second = fills(c, p)
                scores(c, p)
                fill(after_scores)
                if u:
                    project_out(*divmod(u - 1, PAIRS), 0)
                fill(before_first)
                if u == UNITS - 1:
                    up(0, 0)
                attend(c, p, 0)
                fill(between)
                if u:
                    project_out(*divmod(u - 1, PAIRS), 1)
                fill(before_second)
                attend(c, p, 1)
            up(0, 1)
            project_out(HALVES - 1, PAIRS - 1, 0)
            project_out(HALVES - 1, PAIRS - 1, 1)
            for h in range(2, HT):
                up(0, h)
                if h in (2, 4):
                    transform(h - 2)
                    transform(h - 1)
            for k in range(KD):
                pe.wait_ge(t_free, W2_TILES - KD + k + 1)
                transpose_norm(t_bank[k], t_full, 3, k)
            for tiles in ((0, 1), (2, 3)):
                for h in range(HT):
                    down(0, h, tiles)
            for h in range(HT + 2):
                if h < HT:
                    up(1, h)
                if h >= 2:
                    down(1, h - 2, range(TT))

        @block.scalar
        def _(act):
            def high_weights(n):
                _, _, at = CHUNKS[n]
                act.wait_ge(w_loaded[n % 2], 16 * (n // 2 + 1))
                if n >= CHUNK_NO[("w1", 0)]:
                    i = (at - AT_Q) // CH
                    act.wait_ge(lin_full, LIN_NO[("Q", 1, 4 * i + 3)] + 1)
                act.activation(w_hi[:, at:at + CH], w_raw[:, n % 2, :], ACT.Copy).then_inc(w_hi_done, 1)

            def high_x(i, k):
                n = LIN_NO[("X", i, k)]
                act.wait_ge(lin_full, n + 1)
                act.activation(xt_hi[:, k, :], lin_bank[n % 2][:], ACT.Copy).then_inc(x_hi_done, 1)

            def high_v(c, t):
                n = LIN_NO[("V", c, t)]
                act.wait_ge(lin_full, n + 1)
                act.activation(v_hi[:, t, :, :].rearrange("p g e -> p (g e)"), lin_bank[n % 2][:],
                               ACT.Copy).then_inc(v_hi_done, 1)

            def swap(item):
                n, r = LIN_NO[item], ROPE_NO[item]
                act.wait_ge(lin_full, n + 1)
                if r >= 2:
                    act.wait_ge(rope_sum, r - 1)
                h = P // 2
                act.activation(rope_b[0:h, r % 2, :], lin_bank[n % 2][h:P], ACT.Copy)
                act.activation(rope_b[h:P, r % 2, :], lin_bank[n % 2][0:h], ACT.Copy).then_inc(swapped, 1)

            def high_rope(item):
                r = ROPE_NO[item]
                act.wait_ge(rope_sum, r + 1)
                act.activation(rope_dst(item)[0], qk[:, r % 2, :], ACT.Copy).then_inc(rope_hi, 1)

            def high_p(u, s):
                n = 3 * u + s
                act.wait_ge(mask_done, n + 1)
                act.activation(p_hi[:, s, :], p_raw[:, n % 2, :], ACT.Copy).then_inc(p_hi_done, 1)

            def high_o(u, b):
                act.wait_ge(o_full, 2 * u + b + 1)
                act.activation(o_hi[:, b, :, :].rearrange("p h t -> p (h t)"), o_bank[:],
                               ACT.Copy).then_inc(o_hi_done, 1)

            def silu(n):
                act.wait_ge(up_full, n + 1)
                if n >= 2:
                    act.wait_ge(hid_done, n - 1)
                act.activation(rope_a[:, n % 2, :], up_bank[n % 2][0][:], ACT.Silu).then_inc(silu_done, 1)

            def high_hid(n):
                act.wait_ge(hid_done, n + 1)
                if n == 0:
                    act.wait_ge(o_full, 2 * UNITS)
                act.activation(hid_hi[:, n % HT, :], rope_b[:, n % 2, :], ACT.Copy).then_inc(hid_hi_done, 1)

            def high_w2(dc):
                _, _, at = CHUNKS[CHUNK_NO[("w2", dc)]]
                act.wait_ge(fly_done, 3 * (dc + 1))
                act.activation(w_hi[:, at:at + CH], xn_flat, ACT.Copy).then_inc(w2_hi_done, 1)

            def high_t(m):
                act.wait_ge(t_full, m + 1)
                dst = w2_part(w_hi, m) if m < W2_TILES else xt_hi[:, m - W2_TILES, :]
                act.activation(dst, t_bank[m % 2][:], ACT.Copy).then_inc(t_hi_done, 1)

            def fill(*lists):
                for items in lists:
                    for item in items:
                        if item[0] == "X":
                            high_x(*item[1:])
                        elif item[0] == "V":
                            high_v(*item[1:])
                        else:
                            swap(item)

            def fill_rope(*lists):
                for items in lists:
                    for item in items:
                        if item[0] in "KQ" and ROPE_NO[item] > FIRST_ROPE:
                            high_rope(ROPE[ROPE_NO[item] - 1])

            act.dma_start(ident_sb[:], ident).then_inc(tables_loaded, 16)
            act.dma_start(cos_sb[:], cos).then_inc(tables_loaded, 16)
            act.dma_start(sin_sb[:], sin).then_inc(tables_loaded, 16)
            high_weights(0)
            high_x(0, 0)
            high_x(0, 1)
            high_weights(1)
            swap(("K", 0, 0))
            swap(("Q", 0, 0))
            high_rope(("K", 0, 0))
            swap(("Q", 0, 1))
            high_weights(2)
            high_rope(("Q", 0, 0))
            fill(START[5:7])
            high_rope(("Q", 0, 1))
            fill(START[7:])
            high_weights(3)
            for u in range(UNITS):
                c, p = divmod(u, PAIRS)
                after_scores, before_first, between, before_second = fills(c, p)
                for s in range(3):
                    high_p(u, s)
                if u == UNITS - 2:
                    high_rope(ROPE[-1])
                fill(after_scores)
                if unit_chunk(c, p) is not None:
                    high_weights(unit_chunk(c, p))
                fill(before_first)
                if u == UNITS - 1:
                    high_w2(0)
                fill_rope(after_scores, before_first)
                high_o(u, 0)
                if u == UNITS - 1:
                    silu(0)
                fill(between)
                fill_rope(between)
                fill(before_second)
                high_o(u, 1)
                fill_rope(before_second)
            high_hid(0)
            silu(1)
            high_hid(1)
            act.wait_ge(had_loaded, 16)
            act.activation(had[:], had_raw[:], ACT.Copy).then_inc(had_done, 1)
            silu(2)
            high_hid(2)
            high_w2(1)
            for n in range(3, HALVES * HT):
                silu(n)
                high_hid(n)
                if n in (3, 5):
                    high_t(n - 3)
                    high_t(n - 2)
                if n == 7:
                    high_t(4)
                    high_t(5)

        @block.gpsimd
        def _(pool):
            def inverse_deviation(i):
                pool.wait_ge(eps_done, i + 1)
                pool.tensor_tensor(rstd[:], var_eps[:], minus_half[:], ALU.pow).then_inc(rstd_done, 1)

            def rope_add(item):
                r = ROPE_NO[item]
                pool.wait_ge(rope_parts, r + 1)
                if r >= 2:
                    pool.wait_ge(rope_lo, r - 1)
                pool.tensor_tensor(qk[:, r % 2, :], rope_a[:, r % 2, :], rope_b[:, r % 2, :],
                                   ALU.add).then_inc(rope_sum, 1)

            def low_rope(item):
                r = ROPE_NO[item]
                hi, lo = rope_dst(item)
                pool.wait_ge(rope_hi, r + 1)
                pool.tensor_tensor(lo, qk[:, r % 2, :], hi.bitcast(F32), ALU.subtract).then_inc(rope_lo, 1)

            def low_p(u, s):
                n = 3 * u + s
                pool.wait_ge(p_hi_done, n + 1)
                pool.tensor_tensor(p_lo[:, s, :], p_raw[:, n % 2, :], p_hi[:, s, :].bitcast(F32),
                                   ALU.subtract).then_inc(p_lo_pool, 1)

            def low_hid(n):
                pool.wait_ge(hid_hi_done, n + 1)
                pool.tensor_tensor(hid_lo[:, n % HT, :], rope_b[:, n % 2, :], hid_hi[:, n % HT, :].bitcast(F32),
                                   ALU.subtract).then_inc(hid_lo_done, 1)

            def butterfly(dc, step):
                n = CHUNK_NO[("w2", dc)]
                if step:
                    pool.wait_ge(fly_done, 3 * dc + step)
                else:
                    pool.wait_ge(w_loaded[n % 2], 16 * (n // 2 + 1))
                    if dc:
                        pool.wait_ge(w2_lo_done, dc)
                    else:
                        pool.wait_ge(lin_full, LIN_NO[("X", 2, KD - 1)] + 1)
                src, dst = w_raw[:, n % 2, :], xn_flat
                if step == 1:
                    src, dst = dst, src
                s, d = (a.rearrange("p (m two r) -> p m two r", m=1 << step, two=2) for a in (src, dst))
                pool.tensor_tensor(d[:, :, 0, :], s[:, :, 0, :], s[:, :, 1, :], ALU.add)
                pool.tensor_tensor(d[:, :, 1, :], s[:, :, 0, :], s[:, :, 1, :], ALU.subtract).then_inc(fly_done, 1)

            pool.memset(minus_half[:], -0.5).then_inc(half_set, 1)
            pool.wait_ge(half_set, 1)
            inverse_deviation(0)
            for item in ROPE[:FIRST_ROPE]:
                rope_add(item)
                if ROPE_NO[item]:
                    low_rope(ROPE[ROPE_NO[item] - 1])
            low_rope(ROPE[FIRST_ROPE - 1])
            for u in range(UNITS):
                c, p = divmod(u, PAIRS)
                low_p(u, S_FIRST1)
                for item in (i for f in fills(c, p) for i in f if i[0] in "KQ"):
                    rope_add(item)
                    if ROPE_NO[item] > FIRST_ROPE:
                        low_rope(ROPE[ROPE_NO[item] - 1])
                if p == 3:
                    inverse_deviation(c + 1)
                if u == UNITS - 2:
                    low_rope(ROPE[-1])
                if u >= UNITS - 2:
                    for step in range(3):
                        butterfly(u - UNITS + 2, step)
            for n in range(HALVES * HT):
                low_hid(n)
                if n == 2:
                    inverse_deviation(3)

        @block.vector
        def _(dve):
            def norm_stats(i):
                half = i % HALVES
                if i < HALVES:
                    dve.wait_ge(x_loaded[half], 16)
                else:
                    dve.wait_ge(x2_done, BH * (half + 1))
                for t in range(TT):
                    dve.bn_stats(stats[:, t, :], x_sb[:, half * TT + t, :]).then_inc(stats_done, 1)
                for t in range(TT):
                    dve.wait_ge(stats_done, TT * i + t + 1)
                    dve.bn_aggr(mean_var[:, t, :], stats[:, t, :]).then_inc(mv_done, 1)
                dve.wait_ge(mv_done, TT * (i + 1))
                dve.tensor_scalar(var_eps[:], mean_var[:, :, 1], EPS, None, ALU.add).then_inc(eps_done, 1)

            def norm_apply(i):
                half = i % HALVES
                dve.wait_ge(rstd_done, i + 1)
                if i:
                    dve.wait_ge(lin_full, LIN_NO[("X", i - 1, KD - 1)] + 1)
                if i == 3:
                    dve.wait_ge(w2_lo_done, 2)
                for t in range(TT):
                    dve.tensor_scalar(xn[:, t, :], x_sb[:, half * TT + t, :], mean_var[:, t, 0:1], rstd[:, t:t + 1],
                                      ALU.subtract, ALU.mult).then_inc(xn_done, 1)

            def low_weights(n):
                _, _, at = CHUNKS[n]
                dve.wait_ge(w_hi_done, n + 1)
                dve.tensor_tensor(w_lo[:, at:at + CH], w_raw[:, n % 2, :], w_hi[:, at:at + CH].bitcast(F32),
                                  ALU.subtract).then_inc(w_lo_done, 1)

            def low_x(i, k):
                n = LIN_NO[("X", i, k)]
                dve.wait_ge(x_hi_done, X_NO[("X", i, k)] + 1)
                dve.tensor_tensor(xt_lo[:, k, :], lin_bank[n % 2][:], xt_hi[:, k, :].bitcast(F32),
                                  ALU.subtract).then_inc(lin_free, 1)

            def low_v(c, t):
                n = LIN_NO[("V", c, t)]
                dve.wait_ge(v_hi_done, V_NO[("V", c, t)] + 1)
                dve.tensor_tensor(v_lo[:, t, :, :].rearrange("p g e -> p (g e)"), lin_bank[n % 2][:],
                                  v_hi[:, t, :, :].rearrange("p g e -> p (g e)").bitcast(F32),
                                  ALU.subtract).then_inc(lin_free, 1)

            def rotate(item):
                n, r = LIN_NO[item], ROPE_NO[item]
                dve.wait_ge(swapped, r + 1)
                if r >= 2:
                    dve.wait_ge(rope_sum, r - 1)
                src, a, b = (m.rearrange("p (b t) -> p b t", b=BH)
                             for m in (lin_bank[n % 2][:], rope_a[:, r % 2, :], rope_b[:, r % 2, :]))
                c, s = (tb[:].unsqueeze(1).broadcast_to([P, BH, SEQ]) for tb in (cos_sb, sin_sb))
                dve.tensor_tensor(a, src, c, ALU.mult).then_inc(lin_free, 1)
                dve.tensor_tensor(b, b, s, ALU.mult).then_inc(rope_parts, 1)

            def mask(c, p, s):
                u = c * PAIRS + p
                n = 3 * u + s
                dve.wait_ge(s_full, n + 1)
                if c == 0 and p % 2 == 0:
                    dve.wait_ge(decay_loaded[p // 2], 16)
                if s == S_FIRST1:
                    dve.wait_ge(p_lo_dve, 2 * u + 1)
                elif u and s == S_FIRST0:
                    dve.wait_ge(p_lo_dve, 2 * u)
                elif u:
                    dve.wait_ge(p_lo_pool, u)
                table = decay_sb[:, 2 * p:2 * p + 2, :]
                if s == S_SECOND:
                    table = table[:, :, 0:P].unsqueeze(1).broadcast_to([P, BH, 2, P])
                    src = s_bank[s][:].rearrange("p (b h t) -> p b h t", b=BH, h=2)
                    dst = p_raw[:, n % 2, :].rearrange("p (b h t) -> p b h t", b=BH, h=2)
                else:
                    src = s_bank[s][:].rearrange("p (h t) -> p h t", h=2)
                    dst = p_raw[:, n % 2, :].rearrange("p (h t) -> p h t", h=2)
                dve.tensor_tensor(dst, src, table, ALU.mult).then_inc(mask_done, 1)

            def low_p(u, s):
                n = 3 * u + s
                dve.wait_ge(p_hi_done, n + 1)
                dve.tensor_tensor(p_lo[:, s, :], p_raw[:, n % 2, :], p_hi[:, s, :].bitcast(F32),
                                  ALU.subtract).then_inc(p_lo_dve, 1)

            def low_o(u, b):
                dve.wait_ge(o_hi_done, 2 * u + b + 1)
                dve.tensor_tensor(o_lo[:, b, :, :].rearrange("p h t -> p (h t)"), o_bank[:],
                                  o_hi[:, b, :, :].rearrange("p h t -> p (h t)").bitcast(F32),
                                  ALU.subtract).then_inc(o_lo_done, 1)

            def add_attention(c):
                for b in range(BH):
                    dve.wait_ge(y_full, BH * c + b + 1)
                    tiles = x_sb[:, c * TT + 2 * b:c * TT + 2 * b + 2, :]
                    dve.tensor_tensor(tiles, y_bank[b][:].rearrange("p (t d) -> p t d", t=2), tiles,
                                      ALU.add).then_inc(x2_done, 1)

            def hidden(n):
                dve.wait_ge(silu_done, n + 1)
                if n >= 2:
                    dve.wait_ge(hid_lo_done, n - 1)
                dve.tensor_tensor(rope_b[:, n % 2, :], up_bank[n % 2][1][:], rope_a[:, n % 2, :],
                                  ALU.mult).then_inc(hid_done, 1)

            def low_w2(dc):
                _, _, at = CHUNKS[CHUNK_NO[("w2", dc)]]
                dve.wait_ge(w2_hi_done, dc + 1)
                dve.tensor_tensor(w_lo[:, at:at + CH], xn_flat, w_hi[:, at:at + CH].bitcast(F32),
                                  ALU.subtract).then_inc(w2_lo_done, 1)

            def low_t(m):
                dve.wait_ge(t_hi_done, m + 1)
                if m < W2_TILES:
                    dst, hi = w2_part(w_lo, m), w2_part(w_hi, m)
                else:
                    dst, hi = xt_lo[:, m - W2_TILES, :], xt_hi[:, m - W2_TILES, :]
                dve.tensor_tensor(dst, t_bank[m % 2][:], hi.bitcast(F32), ALU.subtract).then_inc(t_free, 1)

            def finish(n):
                dve.wait_ge(down_full, n + 1)
                dve.tensor_tensor(x_sb[:, n, :], down_bank[n % TT][:, 0:D], x_sb[:, n, :],
                                  ALU.add).then_inc(out_done, 1)

            def fill(*lists):
                for items in lists:
                    for item in items:
                        if item[0] == "X":
                            low_x(*item[1:])
                        elif item[0] == "V":
                            low_v(*item[1:])
                        else:
                            rotate(item)

            norm_stats(0)
            low_weights(0)
            norm_apply(0)
            low_x(0, 0)
            low_x(0, 1)
            low_weights(1)
            dve.wait_ge(tables_loaded, 48)
            rotate(("K", 0, 0))
            rotate(("Q", 0, 0))
            low_weights(2)
            rotate(("Q", 0, 1))
            fill(START[5:])
            low_weights(3)
            for u in range(UNITS):
                c, p = divmod(u, PAIRS)
                after_scores, before_first, between, before_second = fills(c, p)
                mask(c, p, S_FIRST0)
                mask(c, p, S_SECOND)
                low_p(u, S_FIRST0)
                if u:
                    low_o(u - 1, 1)
                low_p(u, S_SECOND)
                mask(c, p, S_FIRST1)
                fill(after_scores)
                if unit_chunk(c, p) is not None:
                    low_weights(unit_chunk(c, p))
                fill(before_first)
                if u == UNITS - 1:
                    low_w2(0)
                low_o(u, 0)
                if u == UNITS - 1:
                    hidden(0)
                if p == 3:
                    norm_stats(c + 1)
                if p == 4:
                    norm_apply(c + 1)
                fill(between)
                if u == PAIRS:
                    add_attention(0)
                fill(before_second)
            low_o(UNITS - 1, 1)
            hidden(1)
            add_attention(1)
            norm_stats(3)
            hidden(2)
            low_w2(1)
            hidden(3)
            norm_apply(3)
            low_t(0)
            low_t(1)
            hidden(4)
            hidden(5)
            low_t(2)
            low_t(3)
            hidden(6)
            hidden(7)
            low_t(4)
            low_t(5)
            for n in range(TT):
                finish(n)
            for n in range(HT, 2 * HT):
                hidden(n)
            for n in range(TT, 2 * TT):
                finish(n)


def tables():
    f = np.float32
    inv_freq = f(1.0) / f(10000.0) ** (np.arange(0, P, 2, dtype=f) / f(P))
    angle = (np.arange(SEQ, dtype=f)[None, :] * inv_freq[:, None]).astype(f).astype(np.float64)
    cos = np.concatenate([np.cos(angle)] * 2).astype(f)
    sin = np.concatenate([-np.sin(angle), np.sin(angle)]).astype(f)
    lam = np.exp2(f(-8.0) * np.arange(1, HEADS + 1, dtype=f) / f(HEADS)).astype(np.float64)
    lag = np.arange(SEQ)[None, :] - np.arange(P)[:, None]
    decay = np.where(lag[:, None, :] >= 0, np.exp(-lam[None, :, None] * np.maximum(lag, 0)[:, None, :]), 0.0)
    decay = decay.astype(f).reshape(P, 4, 4, SEQ).transpose(1, 0, 2, 3)
    signs = np.array([[-1.0 if bin(i & j).count("1") % 2 else 1.0 for j in range(P)] for i in range(P)])
    return {"cos": cos, "sin": sin, "decay": decay, "ident": np.eye(P, dtype=f),
            "hadamard": (signs / np.sqrt(HID)).astype(f)}


def layouts(x, wq, wk, wv, wo, w1, w2, w3):
    def stationary(w):
        r = w.reshape(-1, 4, P, KD, P).transpose(0, 4, 1, 3, 2)
        return r.reshape(-1, P, 4 * KD * P)
    return {
        "x": x.reshape(HALVES, TT, P, D).transpose(0, 2, 1, 3),
        "wk": stationary(wk),
        "wv": wv.reshape(1, KVH * P, KD, P).transpose(0, 3, 2, 1).reshape(1, P, CH),
        "wq": stationary(wq),
        "wo": wo.reshape(D, 4, 4, P).transpose(1, 3, 2, 0).reshape(4, P, CH),
        "w1": stationary(w1),
        "w3": stationary(w3),
        "w2": w2.reshape(2, P, HT, P).transpose(0, 3, 2, 1).reshape(2, P, CH),
    }


def kernel(L0_attn_x, L0_attn_wq, L0_attn_wk, L0_attn_wv, L0_attn_wo, L0_ffn_W1, L0_ffn_W2, L0_ffn_W3):
    import concourse.bacc as bacc
    from concourse.bass_utils import run_bass_kernel_spmd

    laid = layouts(*(np.asarray(a) for a in (L0_attn_x, L0_attn_wq, L0_attn_wk, L0_attn_wv, L0_attn_wo,
                                              L0_ffn_W1, L0_ffn_W2, L0_ffn_W3)))
    laid.update(tables())
    nc = bacc.Bacc("TRN2", target_bir_lowering=False, num_devices=1)
    arrays, args = {}, {}
    for name, a in laid.items():
        a = np.ascontiguousarray(a)
        arrays[f"in_{name}"] = a
        args[name] = nc.dram_tensor(f"in_{name}", a.shape, mybir.dt.from_np(a.dtype), kind="ExternalInput").ap()
    out = nc.dram_tensor("out", (HALVES * TT, P, D), F32, kind="ExternalOutput").ap()
    build(nc, out=out, **args)
    r = run_bass_kernel_spmd(nc, [arrays], core_ids=[0])
    return r.results[0]["out"].reshape(NSEQ, SEQ, D)
```

```python
from contextlib import ExitStack

import numpy as np

import concourse.bass as bass
from concourse import mybir

F32 = mybir.dt.float32
F32R = mybir.dt.float32r
ALU = mybir.AluOpType
ACT = mybir.ActivationFunctionType

P = 128
D = 256
KD = D // P
SEQ = 256
NSEQ = 4
HALVES = 2
TOK = NSEQ * SEQ // HALVES
BH = TOK // SEQ
TT = TOK // P
HEADS = 16
KVH = 4
PAIRS = HEADS // 2
PPG = PAIRS // KVH
HID = 1024
HT = HID // P
EPS = 1e-5
UNITS = HALVES * PAIRS

CH = 1024
AT_K, AT_V, AT_Q, AT_O = 0, CH, 2 * CH, 6 * CH
W_COLS = 10 * CH
AT_W2 = AT_K
AT_FF = AT_Q
CHUNKS = [("wk", 0, AT_K), ("wq", 0, AT_Q), ("wv", 0, AT_V), ("wq", 1, AT_Q + CH), ("wo", 0, AT_O),
          ("wq", 2, AT_Q + 2 * CH), ("wo", 1, AT_O + CH), ("wq", 3, AT_Q + 3 * CH), ("wo", 2, AT_O + 2 * CH),
          ("wo", 3, AT_O + 3 * CH),
          ("w1", 0, AT_FF), ("w3", 0, AT_FF + CH), ("w1", 1, AT_FF + 2 * CH), ("w3", 1, AT_FF + 3 * CH),
          ("w2", 0, AT_W2), ("w2", 1, AT_W2 + CH)]
CHUNK_NO = {(w, i): n for n, (w, i, _) in enumerate(CHUNKS)}
SLOTS = 3
FIRST_CHUNKS = 4

START = ([("X", 0, k) for k in range(KD)] + [("K", 0, 0), ("Q", 0, 0), ("V", 0, 0), ("Q", 0, 1), ("V", 0, 1),
          ("Q", 0, 2), ("V", 0, 2), ("Q", 0, 3), ("V", 0, 3)])


def queries(u):
    c, p = divmod(u + 2, PAIRS)
    return [("Q", c, 2 * p), ("Q", c, 2 * p + 1)] if u + 2 < UNITS else []


def key(u):
    c, p = divmod(u + 2, PAIRS)
    return [("K", c, p // PPG)] if 0 <= u < UNITS - 2 and p % PPG == 0 else []


def values(u):
    return [("V", 1, t) for t in range(TT)] if u == PAIRS else []


def turned(u):
    c, p = divmod(u, PAIRS)
    return [("X", c + 1, k) for k in range(KD)] if p == PAIRS - 3 else []


def unit_chunk(u):
    if u < PAIRS:
        return FIRST_CHUNKS + u if FIRST_CHUNKS + u < CHUNK_NO[("w1", 0)] else None
    return {9: CHUNK_NO[("w1", 0)], 11: CHUNK_NO[("w3", 0)],
            12: CHUNK_NO[("w1", 1)], 13: CHUNK_NO[("w3", 1)]}.get(u)


LIN = START + [i for u in range(UNITS) for i in values(u)[:2] + queries(u) + values(u)[2:] + key(u) + turned(u)]
LIN_NO = {item: n for n, item in enumerate(LIN)}
ROPE = [i for i in LIN if i[0] in "KQ"]
ROPE_NO = {item: n for n, item in enumerate(ROPE)}
V_NO = {item: n for n, item in enumerate(i for i in LIN if i[0] == "V")}
X_NO = {item: n for n, item in enumerate(i for i in LIN if i[0] == "X")}

S_FIRST0, S_SECOND, S_FIRST1 = range(3)
S_OF_SEQ = (S_FIRST0, S_FIRST1)
W2_TILES = 4


def build(nc, x, wk, wv, wq, wo, w1, w3, w2, cos, sin, decay, ident, hadamard, out):
    dram = {"wk": wk, "wv": wv, "wq": wq, "wo": wo, "w1": w1, "w3": w3, "w2": w2}

    with ExitStack() as ctx:
        def sb(name, shape, dt=F32):
            return ctx.enter_context(nc.sbuf_tensor(name, shape, dt))

        def sem(name):
            return ctx.enter_context(nc.semaphore(name))

        w_hi = sb("w_hi", [P, W_COLS], F32R)
        w_lo = sb("w_lo", [P, W_COLS], F32R)
        w_raw = sb("w_raw", [P, SLOTS, CH])
        x_sb = sb("x_sb", [P, HALVES * TT, D])
        xn = sb("xn", [P, TT, D])
        xt_hi = sb("xt_hi", [P, KD, TOK], F32R)
        xt_lo = sb("xt_lo", [P, KD, TOK], F32R)
        k_hi = sb("k_hi", [P, 2, TOK], F32R)
        k_lo = sb("k_lo", [P, 2, TOK], F32R)
        v_hid = sb("v_hid", [P, 2, TT * KVH * P], F32R)
        q_hid = sb("q_hid", [P, 2, 2 * 2 * TOK], F32R)
        rope_a = sb("rope_a", [P, 2, TOK])
        rope_b = sb("rope_b", [P, 2, TOK])
        qk = sb("qk", [P, 2, TOK])
        p_raw = sb("p_raw", [P, 2, TOK])
        p_hi = sb("p_hi", [P, 3, TOK], F32R)
        p_lo = sb("p_lo", [P, 3, TOK], F32R)
        o_hi = sb("o_hi", [P, BH, 2, SEQ], F32R)
        o_lo = sb("o_lo", [P, BH, 2, SEQ], F32R)
        cos_sb = sb("cos_sb", [P, SEQ])
        sin_sb = sb("sin_sb", [P, SEQ])
        decay_sb = sb("decay_sb", [P, HEADS, SEQ])
        ident_sb = sb("ident_sb", [P, P])
        had_raw = sb("had_raw", [P, P])
        had = sb("had", [P, P], F32R)
        stats = sb("stats", [P, TT, 6])
        mean_var = sb("mean_var", [P, TT, 2])
        var_eps = sb("var_eps", [P, TT])
        rstd = sb("rstd", [P, TT])
        minus_half = sb("minus_half", [P, TT])

        bank = [ctx.enter_context(nc.psum_tensor(f"bank{i}", [P, 512], F32)) for i in range(8)]
        s_bank = bank[2:5]
        o_bank = bank[5]
        y_bank = bank[6:8]
        up_bank = (bank[0:2], bank[2:4])
        t_bank = bank[4:6]
        down_bank = (bank[6], bank[7], bank[4], bank[5])

        v_hi = v_hid[:, 0, :].rearrange("p (t g e) -> p t g e", t=TT, g=KVH)
        v_lo = v_hid[:, 1, :].rearrange("p (t g e) -> p t g e", t=TT, g=KVH)
        q_hi = q_hid[:, 0, :].rearrange("p (s h t) -> p s h t", s=2, h=2)
        q_lo = q_hid[:, 1, :].rearrange("p (s h t) -> p s h t", s=2, h=2)
        hid_hi = v_hid[:, :, :].rearrange("p a (h t) -> p (a h) t", t=TOK)
        hid_lo = q_hid[:, :, :].rearrange("p a (h t) -> p (a h) t", t=TOK)
        xn_flat = xn[:, :, :].rearrange("p t d -> p (t d)")

        x_loaded = [sem(f"x_loaded{i}") for i in range(NSEQ)]
        tables_loaded = sem("tables_loaded")
        decay_loaded = [sem(f"decay_loaded{i}") for i in range(4)]
        had_loaded = sem("had_loaded")
        w_loaded = [sem(f"w_loaded{s}") for s in range(SLOTS)]
        stored = sem("stored")
        w_hi_done, w_lo_done, had_done = sem("w_hi_done"), sem("w_lo_done"), sem("had_done")
        stats_done, mv_done, eps_done = sem("stats_done"), sem("mv_done"), sem("eps_done")
        half_set, rstd_done, xn_done = sem("half_set"), sem("rstd_done"), sem("xn_done")
        lin_full, lin_free = sem("lin_full"), sem("lin_free")
        x_hi_done, v_hi_done = sem("x_hi_done"), sem("v_hi_done")
        swapped, rope_parts, rope_sum = sem("swapped"), sem("rope_parts"), sem("rope_sum")
        rope_hi, rope_lo = sem("rope_hi"), sem("rope_lo")
        s_full, mask_done, p_hi_done = sem("s_full"), sem("mask_done"), sem("p_hi_done")
        p_lo_dve, p_lo_pool = sem("p_lo_dve"), sem("p_lo_pool")
        o_full, o_hi_done, o_lo_done = sem("o_full"), sem("o_hi_done"), sem("o_lo_done")
        y_full, x2_done = sem("y_full"), sem("x2_done")
        up_full, silu_done, hid_done = sem("up_full"), sem("silu_done"), sem("hid_done")
        hid_hi_done, hid_lo_done = sem("hid_hi_done"), sem("hid_lo_done")
        fly_done, w2_hi_done, w2_lo_done = sem("fly_done"), sem("w2_hi_done"), sem("w2_lo_done")
        t_full, t_hi_done, t_free = sem("t_full"), sem("t_hi_done"), sem("t_free")
        down_full, out_done = sem("down_full"), sem("out_done")

        block = ctx.enter_context(nc.Block())

        def lin_bank(n):
            return bank[n] if n < len(bank) else bank[n % 2]

        def rope_dst(item):
            kind, _, n = item
            if kind == "K":
                return k_hi[:, n % 2, :], k_lo[:, n % 2, :]
            return q_hi[:, n // 2 % 2, n % 2, :], q_lo[:, n // 2 % 2, n % 2, :]

        def w2_part(w, m):
            return w[:, AT_W2 + m * 512:AT_W2 + (m + 1) * 512]

        def w2_tile(w, h):
            return w[:, AT_W2:AT_W2 + 2 * CH].rearrange("p (c a d) -> p c a d", c=2, a=HT)[:, :, h, :]

        @block.sync
        def _(sp):
            def load_chunk(n):
                if n >= SLOTS:
                    sp.wait_ge(w_lo_done, n - SLOTS + 1)
                w, i, _ = CHUNKS[n]
                sp.dma_start(w_raw[:, n % SLOTS, :], dram[w][i]).then_inc(w_loaded[n % SLOTS], 16)

            def load_x(c):
                for i in range(BH * c, BH * (c + 1)):
                    sp.dma_start(x_sb[:, 2 * i:2 * i + 2, :], x[i]).then_inc(x_loaded[i], 16)

            def load_decay(i):
                sp.dma_start(decay_sb[:, 4 * i:4 * i + 4, :], decay[i]).then_inc(decay_loaded[i], 16)

            load_x(0)
            for n in range(3):
                load_chunk(n)
            load_chunk(3)
            load_decay(0)
            load_chunk(4)
            load_decay(1)
            load_x(1)
            load_chunk(5)
            load_decay(2)
            load_decay(3)
            sp.dma_start(had_raw[:], hadamard).then_inc(had_loaded, 16)
            for n in range(6, len(CHUNKS)):
                load_chunk(n)
            for n in range(HALVES * TT):
                sp.wait_ge(out_done, n + 1)
                sp.dma_start(out[n], x_sb[:, n, :]).then_inc(stored, 16)
            sp.wait_ge(stored, 16 * HALVES * TT)

        @block.tensor
        def _(pe):
            def product(o, a_hi, a_lo, b_hi, b_lo, first, last, shared=False):
                pe.matmul(o, a_hi, b_hi, start=first, stop=False, skip_group_check=shared)
                pe.matmul(o, a_hi, b_lo, start=False, stop=False, skip_group_check=shared)
                return pe.matmul(o, a_lo, b_hi, start=False, stop=last, skip_group_check=shared)

            def lin_wait(item):
                n = LIN_NO[item]
                if n >= len(bank):
                    pe.wait_ge(lin_free, (n - 2 if n >= len(bank) + 2 else n - len(bank)) + 1)
                return lin_bank(n)

            def transpose_norm(dst, full, i, k):
                for t in range(TT):
                    pe.wait_ge(xn_done, TT * i + t + 1)
                    last = pe.transpose(dst[:, t * P:(t + 1) * P], xn[:, t, k * P:(k + 1) * P], ident_sb[:])
                last.then_inc(full, 1)

            def turn(i, k):
                transpose_norm(lin_wait(("X", i, k)), lin_full, i, k)

            def project(item):
                kind, c, h = item
                o = lin_wait(item)
                chunk = ("wk", 0) if kind == "K" else ("wq", h // 4)
                pe.wait_ge(w_lo_done, CHUNK_NO[chunk] + 1)
                at = (AT_K if kind == "K" else AT_Q) + h * KD * P
                for k in range(KD):
                    pe.wait_ge(lin_free, LIN_NO[("X", c, k)] + 1)
                    a = slice(at + k * P, at + (k + 1) * P)
                    last = product(o[:], w_hi[:, a], w_lo[:, a], xt_hi[:, k, :], xt_lo[:, k, :],
                                   k == 0, k == KD - 1)
                last.then_inc(lin_full, 1)

            def project_values(c, t):
                o = lin_wait(("V", c, t))
                pe.wait_ge(lin_free, LIN_NO[("X", c, KD - 1)] + 1)
                pe.wait_ge(w_lo_done, CHUNK_NO[("wv", 0)] + 1)
                for k in range(KD):
                    a, b = slice(t * P, (t + 1) * P), slice(AT_V + k * 512, AT_V + (k + 1) * 512)
                    last = product(o[:], xt_hi[:, k, a], xt_lo[:, k, a], w_hi[:, b], w_lo[:, b],
                                   k == 0, k == KD - 1)
                last.then_inc(lin_full, 1)

            def scores(u, s):
                c, p = divmod(u, PAIRS)
                ks, qs = p // PPG % 2, p % 2
                needed = max(ROPE_NO[("Q", c, 2 * p + 1)], ROPE_NO[("K", c, p // PPG)])
                pe.wait_ge(rope_lo, needed + 1)
                if u:
                    pe.wait_ge(mask_done, 3 * (u - 1) + s + 1)
                if s == S_SECOND:
                    for b in range(BH):
                        a = slice(b * SEQ + P, (b + 1) * SEQ)
                        last = product(s_bank[s][:, b * 256:(b + 1) * 256], k_hi[:, ks, a], k_lo[:, ks, a],
                                       q_hi[:, qs, :, a], q_lo[:, qs, :, a], True, True)
                else:
                    b = S_OF_SEQ.index(s)
                    a, i = slice(b * SEQ, b * SEQ + P), slice(b * SEQ, (b + 1) * SEQ)
                    last = product(s_bank[s][:], k_hi[:, ks, a], k_lo[:, ks, a],
                                   q_hi[:, qs, :, i], q_lo[:, qs, :, i], True, True)
                last.then_inc(s_full, 1)

            def attend(u, b):
                c, p = divmod(u, PAIRS)
                g = p // PPG
                if b == 0:
                    pe.wait_ge(p_lo_dve, 2 * (u + 1))
                else:
                    pe.wait_ge(p_lo_pool, u + 1)
                pe.wait_ge(lin_free, LIN_NO[("V", c, 2 * b + 1)] + 1)
                if 2 * u + b:
                    pe.wait_ge(o_lo_done, 2 * u + b)
                s = S_OF_SEQ[b]
                product(o_bank[:], v_hi[:, 2 * b, g, :], v_lo[:, 2 * b, g, :], p_hi[:, s, :], p_lo[:, s, :],
                        True, False)
                second = o_bank[:].rearrange("p (h t) -> p h t", h=2)[:, :, P:SEQ]
                a = slice(b * 256, (b + 1) * 256)
                product(second, v_hi[:, 2 * b + 1, g, :], v_lo[:, 2 * b + 1, g, :],
                        p_hi[:, S_SECOND, a], p_lo[:, S_SECOND, a], False, True).then_inc(o_full, 1)

            def project_out(u, b):
                c, p = divmod(u, PAIRS)
                pe.wait_ge(o_lo_done, 2 * u + b + 1)
                pe.wait_ge(w_lo_done, CHUNK_NO[("wo", p // 2)] + 1)
                if c and p == 0:
                    pe.wait_ge(x2_done, BH * (c - 1) + b + 1)
                for h in range(2):
                    w = slice(AT_O + (2 * p + h) * D, AT_O + (2 * p + h + 1) * D)
                    for t in range(2):
                        a = slice(t * P, (t + 1) * P)
                        last = product(y_bank[b][:, t * D:(t + 1) * D], o_hi[:, b, h, a], o_lo[:, b, h, a],
                                       w_hi[:, w], w_lo[:, w], p == 0 and h == 0 and t == 0,
                                       p == PAIRS - 1 and h == 1 and t == 1, shared=True)
                if p == PAIRS - 1:
                    last.then_inc(y_full, 1)

            def up(c, h):
                n = c * HT + h
                pe.wait_ge(w_lo_done, CHUNK_NO[("w3", h // 4)] + 1)
                if n == 0:
                    pe.wait_ge(lin_free, len(LIN))
                if n == 1:
                    pe.wait_ge(mask_done, 3 * UNITS - 1)
                if n >= 2:
                    pe.wait_ge(hid_done, n - 1)
                if c and h == 0:
                    pe.wait_ge(t_free, W2_TILES + KD)
                for j in range(2):
                    at = AT_FF + (h // 4 * 2 + j) * CH + h % 4 * KD * P
                    for k in range(KD):
                        a = slice(at + k * P, at + (k + 1) * P)
                        last = product(up_bank[n % 2][j][:], w_hi[:, a], w_lo[:, a], xt_hi[:, k, :], xt_lo[:, k, :],
                                       k == 0, k == KD - 1)
                last.then_inc(up_full, 1)

            def transform(m):
                pe.wait_ge(w2_lo_done, m // 2 + 1)
                if m == 0:
                    pe.wait_ge(had_done, 1)
                    pe.wait_ge(mask_done, 3 * UNITS)
                elif m == 1:
                    pe.wait_ge(o_lo_done, 2 * UNITS)
                else:
                    pe.wait_ge(t_free, m - 1)
                pe.matmul(t_bank[m % 2][:], had[:], w2_part(w_hi, m), start=True, stop=False)
                pe.matmul(t_bank[m % 2][:], had[:], w2_part(w_lo, m), start=False, stop=True).then_inc(t_full, 1)

            def down(c, h, tiles):
                pe.wait_ge(hid_lo_done, c * HT + h + 1)
                for t in tiles:
                    if h == 0 and c:
                        pe.wait_ge(out_done, t + 1)
                    elif h == 0 and t == 0:
                        pe.wait_ge(x2_done, HALVES * BH)
                        pe.wait_ge(t_free, W2_TILES)
                    elif h == 0 and t == 2:
                        pe.wait_ge(t_free, W2_TILES + KD)
                    a = slice(t * P, (t + 1) * P)
                    last = product(down_bank[t][:, 0:D], hid_hi[:, h, a], hid_lo[:, h, a],
                                   w2_tile(w_hi, h), w2_tile(w_lo, h), h == 0, h == HT - 1)
                    if h == HT - 1:
                        last.then_inc(down_full, 1)

            def fill(items):
                for item in items:
                    if item[0] == "X":
                        turn(*item[1:])
                    elif item[0] == "V":
                        project_values(*item[1:])
                    else:
                        project(item)

            pe.wait_ge(tables_loaded, 48)
            fill(START)
            for u in range(UNITS + 1):
                if u < UNITS:
                    scores(u, S_FIRST0)
                    scores(u, S_SECOND)
                if u == UNITS:
                    up(0, 2)
                if u > 1:
                    project_out(u - 2, 1)
                if u:
                    attend(u - 1, 1)
                if u < UNITS:
                    fill(values(u)[:1])
                    scores(u, S_FIRST1)
                    fill(values(u)[1:2] + queries(u))
                if u:
                    project_out(u - 1, 0)
                if u in (UNITS - 2, UNITS - 1):
                    up(0, u - UNITS + 2)
                if u < UNITS:
                    fill(values(u)[2:3])
                    attend(u, 0)
                    fill(values(u)[3:] + key(u) + turned(u))
            up(0, 3)
            project_out(UNITS - 1, 1)
            for h in range(4, HT):
                up(0, h)
                if h in (4, 6):
                    transform(h - 4)
                    transform(h - 3)
            for k in range(KD):
                pe.wait_ge(t_free, W2_TILES - KD + k + 1)
                transpose_norm(t_bank[k], t_full, 3, k)
            for tiles in ((0, 1), (2, 3)):
                for h in range(HT):
                    down(0, h, tiles)
            for h in range(HT + 3):
                if h < HT:
                    up(1, h)
                if h >= 3:
                    down(1, h - 3, range(TT))

        @block.scalar
        def _(act):
            def high_weights(n):
                _, _, at = CHUNKS[n]
                act.wait_ge(w_loaded[n % SLOTS], 16 * (n // SLOTS + 1))
                if n >= CHUNK_NO[("w1", 0)]:
                    i = (at - AT_Q) // CH
                    act.wait_ge(lin_full, LIN_NO[("Q", 1, 4 * i + 3)] + 1)
                act.activation(w_hi[:, at:at + CH], w_raw[:, n % SLOTS, :], ACT.Copy).then_inc(w_hi_done, 1)

            def high_x(i, k):
                n = LIN_NO[("X", i, k)]
                act.wait_ge(lin_full, n + 1)
                act.activation(xt_hi[:, k, :], lin_bank(n)[:], ACT.Copy).then_inc(x_hi_done, 1)

            def high_v(c, t):
                n = LIN_NO[("V", c, t)]
                act.wait_ge(lin_full, n + 1)
                act.activation(v_hi[:, t, :, :].rearrange("p g e -> p (g e)"), lin_bank(n)[:],
                               ACT.Copy).then_inc(v_hi_done, 1)

            def swap(item):
                n, r = LIN_NO[item], ROPE_NO[item]
                act.wait_ge(lin_full, n + 1)
                if r >= 2:
                    act.wait_ge(rope_sum, r - 1)
                h = P // 2
                act.activation(rope_b[0:h, r % 2, :], lin_bank(n)[h:P], ACT.Copy)
                act.activation(rope_b[h:P, r % 2, :], lin_bank(n)[0:h], ACT.Copy).then_inc(swapped, 1)

            def high_rope(item):
                r = ROPE_NO[item]
                act.wait_ge(rope_sum, r + 1)
                act.activation(rope_dst(item)[0], qk[:, r % 2, :], ACT.Copy).then_inc(rope_hi, 1)

            def high_p(u, s):
                n = 3 * u + s
                act.wait_ge(mask_done, n + 1)
                if u and s == S_SECOND:
                    act.wait_ge(o_full, 2 * u)
                act.activation(p_hi[:, s, :], p_raw[:, n % 2, :], ACT.Copy).then_inc(p_hi_done, 1)

            def high_o(u, b):
                act.wait_ge(o_full, 2 * u + b + 1)
                act.activation(o_hi[:, b, :, :].rearrange("p h t -> p (h t)"), o_bank[:],
                               ACT.Copy).then_inc(o_hi_done, 1)

            def silu(n):
                act.wait_ge(up_full, n + 1)
                if n >= 2:
                    act.wait_ge(hid_done, n - 1)
                act.activation(rope_a[:, n % 2, :], up_bank[n % 2][0][:], ACT.Silu).then_inc(silu_done, 1)

            def high_hid(n):
                act.wait_ge(hid_done, n + 1)
                if n < 4:
                    act.wait_ge(o_full, 2 * UNITS - 1 + n // 2)
                act.activation(hid_hi[:, n % HT, :], rope_b[:, n % 2, :], ACT.Copy).then_inc(hid_hi_done, 1)

            def high_w2(dc):
                _, _, at = CHUNKS[CHUNK_NO[("w2", dc)]]
                act.wait_ge(fly_done, 3 * (dc + 1))
                act.activation(w_hi[:, at:at + CH], xn_flat, ACT.Copy).then_inc(w2_hi_done, 1)

            def high_t(m):
                act.wait_ge(t_full, m + 1)
                dst = w2_part(w_hi, m) if m < W2_TILES else xt_hi[:, m - W2_TILES, :]
                act.activation(dst, t_bank[m % 2][:], ACT.Copy).then_inc(t_hi_done, 1)

            def fill(*lists):
                for items in lists:
                    for item in items:
                        if item[0] == "X":
                            high_x(*item[1:])
                        elif item[0] == "V":
                            high_v(*item[1:])
                        else:
                            swap(item)

            act.dma_start(ident_sb[:], ident).then_inc(tables_loaded, 16)
            act.dma_start(cos_sb[:], cos).then_inc(tables_loaded, 16)
            act.dma_start(sin_sb[:], sin).then_inc(tables_loaded, 16)
            high_weights(0)
            high_x(0, 0)
            high_x(0, 1)
            high_weights(1)
            high_weights(2)
            high_weights(3)
            swap(("K", 0, 0))
            swap(("Q", 0, 0))
            high_v(0, 0)
            high_rope(("K", 0, 0))
            swap(("Q", 0, 1))
            high_v(0, 1)
            high_rope(("Q", 0, 0))
            swap(("Q", 0, 2))
            high_v(0, 2)
            high_rope(("Q", 0, 1))
            swap(("Q", 0, 3))
            high_v(0, 3)
            high_rope(("Q", 0, 2))
            high_p(0, S_FIRST0)
            high_rope(("Q", 0, 3))
            high_p(0, S_SECOND)
            for u in range(UNITS):
                if u:
                    before = queries(u - 1)
                    fill(key(u - 1) + turned(u - 1))
                    for item in before[:1]:
                        high_rope(item)
                    high_p(u, S_FIRST0)
                    for item in before[1:]:
                        high_rope(item)
                    high_o(u - 1, 1)
                    high_p(u, S_SECOND)
                fill(values(u)[:2] + queries(u)[:1])
                for item in key(u - 1):
                    high_rope(item)
                fill(queries(u)[1:])
                high_p(u, S_FIRST1)
                if u in (UNITS - 2, UNITS - 1):
                    silu(u - UNITS + 2)
                fill(values(u)[2:3])
                high_o(u, 0)
                fill(values(u)[3:])
                if unit_chunk(u) is not None:
                    high_weights(unit_chunk(u))
            high_hid(0)
            high_hid(1)
            high_w2(0)
            silu(2)
            high_o(UNITS - 1, 1)
            high_hid(2)
            act.wait_ge(had_loaded, 16)
            act.activation(had[:], had_raw[:], ACT.Copy).then_inc(had_done, 1)
            silu(3)
            high_hid(3)
            high_w2(1)
            for n in range(4, HALVES * HT):
                silu(n)
                if n == 6:
                    high_t(2)
                    high_t(3)
                high_hid(n)
                if n == 4:
                    high_t(0)
                    high_t(1)
                if n == 7:
                    high_t(4)
                    high_t(5)

        @block.gpsimd
        def _(pool):
            def inverse_deviation(i):
                pool.wait_ge(eps_done, i + 1)
                pool.tensor_tensor(rstd[:], var_eps[:], minus_half[:], ALU.pow).then_inc(rstd_done, 1)

            def rope_add(item):
                r = ROPE_NO[item]
                pool.wait_ge(rope_parts, r + 1)
                if r >= 2:
                    pool.wait_ge(rope_lo, r - 1)
                pool.tensor_tensor(qk[:, r % 2, :], rope_a[:, r % 2, :], rope_b[:, r % 2, :],
                                   ALU.add).then_inc(rope_sum, 1)

            def low_rope(item):
                r = ROPE_NO[item]
                hi, lo = rope_dst(item)
                pool.wait_ge(rope_hi, r + 1)
                pool.tensor_tensor(lo, qk[:, r % 2, :], hi.bitcast(F32), ALU.subtract).then_inc(rope_lo, 1)

            def low_p(u, s):
                n = 3 * u + s
                pool.wait_ge(p_hi_done, n + 1)
                pool.tensor_tensor(p_lo[:, s, :], p_raw[:, n % 2, :], p_hi[:, s, :].bitcast(F32),
                                   ALU.subtract).then_inc(p_lo_pool, 1)

            def butterfly(dc, step):
                n = CHUNK_NO[("w2", dc)]
                if step:
                    pool.wait_ge(fly_done, 3 * dc + step)
                else:
                    pool.wait_ge(w_loaded[n % SLOTS], 16 * (n // SLOTS + 1))
                    if dc:
                        pool.wait_ge(w2_lo_done, dc)
                    else:
                        pool.wait_ge(lin_full, LIN_NO[("X", 2, KD - 1)] + 1)
                src, dst = w_raw[:, n % SLOTS, :], xn_flat
                if step == 1:
                    src, dst = dst, src
                s, d = (a.rearrange("p (m two r) -> p m two r", m=1 << step, two=2) for a in (src, dst))
                pool.tensor_tensor(d[:, :, 0, :], s[:, :, 0, :], s[:, :, 1, :], ALU.add)
                pool.tensor_tensor(d[:, :, 1, :], s[:, :, 0, :], s[:, :, 1, :], ALU.subtract).then_inc(fly_done, 1)

            pool.memset(minus_half[:], -0.5).then_inc(half_set, 1)
            pool.wait_ge(half_set, 1)
            inverse_deviation(0)
            rope_add(("K", 0, 0))
            rope_add(("Q", 0, 0))
            low_rope(("K", 0, 0))
            rope_add(("Q", 0, 1))
            low_rope(("Q", 0, 0))
            low_rope(("Q", 0, 1))
            rope_add(("Q", 0, 2))
            rope_add(("Q", 0, 3))
            low_rope(("Q", 0, 2))
            low_rope(("Q", 0, 3))
            for u in range(UNITS):
                if u:
                    before = queries(u - 1)
                    for item in before[:1]:
                        low_rope(item)
                    if u % PAIRS == 3:
                        inverse_deviation(u // PAIRS + 1)
                    for item in key(u - 1):
                        rope_add(item)
                    for item in before[1:] + key(u - 1):
                        low_rope(item)
                low_p(u, S_FIRST1)
                for item in queries(u):
                    rope_add(item)
                if u >= UNITS - 2:
                    for step in range(3):
                        butterfly(u - UNITS + 2, step)
            inverse_deviation(3)

        @block.vector
        def _(dve):
            def tile_stats(i, t):
                half = i % HALVES
                if i >= HALVES:
                    dve.wait_ge(x2_done, BH * half + t // 2 + 1)
                else:
                    dve.wait_ge(x_loaded[BH * half + t // 2], 16)
                if i:
                    dve.wait_ge(mv_done, TT * i)
                dve.bn_stats(stats[:, t, :], x_sb[:, half * TT + t, :]).then_inc(stats_done, 1)

            def norm_variance(i):
                for t in range(TT):
                    dve.wait_ge(stats_done, TT * i + t + 1)
                    dve.bn_aggr(mean_var[:, t, :], stats[:, t, :]).then_inc(mv_done, 1)
                dve.wait_ge(mv_done, TT * (i + 1))
                dve.tensor_scalar(var_eps[:], mean_var[:, :, 1], EPS, None, ALU.add).then_inc(eps_done, 1)

            def norm_apply(i, tiles):
                half = i % HALVES
                dve.wait_ge(rstd_done, i + 1)
                if i:
                    dve.wait_ge(lin_full, LIN_NO[("X", i - 1, KD - 1)] + 1)
                if i == 3:
                    dve.wait_ge(w2_lo_done, 2)
                for t in tiles:
                    dve.tensor_scalar(xn[:, t, :], x_sb[:, half * TT + t, :], mean_var[:, t, 0:1], rstd[:, t:t + 1],
                                      ALU.subtract, ALU.mult).then_inc(xn_done, 1)

            def low_weights(n):
                _, _, at = CHUNKS[n]
                dve.wait_ge(w_hi_done, n + 1)
                dve.tensor_tensor(w_lo[:, at:at + CH], w_raw[:, n % SLOTS, :], w_hi[:, at:at + CH].bitcast(F32),
                                  ALU.subtract).then_inc(w_lo_done, 1)

            def low_x(i, k):
                n = LIN_NO[("X", i, k)]
                dve.wait_ge(x_hi_done, X_NO[("X", i, k)] + 1)
                dve.tensor_tensor(xt_lo[:, k, :], lin_bank(n)[:], xt_hi[:, k, :].bitcast(F32),
                                  ALU.subtract).then_inc(lin_free, 1)

            def low_v(c, t):
                n = LIN_NO[("V", c, t)]
                dve.wait_ge(v_hi_done, V_NO[("V", c, t)] + 1)
                dve.tensor_tensor(v_lo[:, t, :, :].rearrange("p g e -> p (g e)"), lin_bank(n)[:],
                                  v_hi[:, t, :, :].rearrange("p g e -> p (g e)").bitcast(F32),
                                  ALU.subtract).then_inc(lin_free, 1)

            def rotate(item):
                n, r = LIN_NO[item], ROPE_NO[item]
                dve.wait_ge(swapped, r + 1)
                if r >= 2:
                    dve.wait_ge(rope_sum, r - 1)
                src, a, b = (m.rearrange("p (b t) -> p b t", b=BH)
                             for m in (lin_bank(n)[:], rope_a[:, r % 2, :], rope_b[:, r % 2, :]))
                c, s = (tb[:].unsqueeze(1).broadcast_to([P, BH, SEQ]) for tb in (cos_sb, sin_sb))
                dve.tensor_tensor(a, src, c, ALU.mult).then_inc(lin_free, 1)
                dve.tensor_tensor(b, b, s, ALU.mult).then_inc(rope_parts, 1)

            def mask(u, s):
                c, p = divmod(u, PAIRS)
                n = 3 * u + s
                dve.wait_ge(s_full, n + 1)
                if c == 0 and p % 2 == 0:
                    dve.wait_ge(decay_loaded[p // 2], 16)
                if s == S_FIRST1:
                    dve.wait_ge(p_lo_dve, 2 * u + 1)
                elif u and s == S_FIRST0:
                    dve.wait_ge(p_lo_dve, 2 * u)
                elif u:
                    dve.wait_ge(p_lo_pool, u)
                table = decay_sb[:, 2 * p:2 * p + 2, :]
                if s == S_SECOND:
                    table = table[:, :, 0:P].unsqueeze(1).broadcast_to([P, BH, 2, P])
                    src = s_bank[s][:].rearrange("p (b h t) -> p b h t", b=BH, h=2)
                    dst = p_raw[:, n % 2, :].rearrange("p (b h t) -> p b h t", b=BH, h=2)
                else:
                    src = s_bank[s][:].rearrange("p (h t) -> p h t", h=2)
                    dst = p_raw[:, n % 2, :].rearrange("p (h t) -> p h t", h=2)
                dve.tensor_tensor(dst, src, table, ALU.mult).then_inc(mask_done, 1)

            def low_p(u, s):
                n = 3 * u + s
                dve.wait_ge(p_hi_done, n + 1)
                dve.tensor_tensor(p_lo[:, s, :], p_raw[:, n % 2, :], p_hi[:, s, :].bitcast(F32),
                                  ALU.subtract).then_inc(p_lo_dve, 1)

            def low_o(u, b):
                dve.wait_ge(o_hi_done, 2 * u + b + 1)
                dve.tensor_tensor(o_lo[:, b, :, :].rearrange("p h t -> p (h t)"), o_bank[:],
                                  o_hi[:, b, :, :].rearrange("p h t -> p (h t)").bitcast(F32),
                                  ALU.subtract).then_inc(o_lo_done, 1)

            def add_attention(c, b):
                dve.wait_ge(y_full, BH * c + b + 1)
                tiles = x_sb[:, c * TT + 2 * b:c * TT + 2 * b + 2, :]
                dve.tensor_tensor(tiles, y_bank[b][:].rearrange("p (t d) -> p t d", t=2), tiles,
                                  ALU.add).then_inc(x2_done, 1)

            def hidden(n):
                dve.wait_ge(silu_done, n + 1)
                if n >= 2:
                    dve.wait_ge(hid_lo_done, n - 1)
                dve.tensor_tensor(rope_b[:, n % 2, :], up_bank[n % 2][1][:], rope_a[:, n % 2, :],
                                  ALU.mult).then_inc(hid_done, 1)

            def low_hid(n):
                dve.wait_ge(hid_hi_done, n + 1)
                dve.tensor_tensor(hid_lo[:, n % HT, :], rope_b[:, n % 2, :], hid_hi[:, n % HT, :].bitcast(F32),
                                  ALU.subtract).then_inc(hid_lo_done, 1)

            def low_w2(dc):
                _, _, at = CHUNKS[CHUNK_NO[("w2", dc)]]
                dve.wait_ge(w2_hi_done, dc + 1)
                dve.tensor_tensor(w_lo[:, at:at + CH], xn_flat, w_hi[:, at:at + CH].bitcast(F32),
                                  ALU.subtract).then_inc(w2_lo_done, 1)

            def low_t(m):
                dve.wait_ge(t_hi_done, m + 1)
                if m < W2_TILES:
                    dst, hi = w2_part(w_lo, m), w2_part(w_hi, m)
                else:
                    dst, hi = xt_lo[:, m - W2_TILES, :], xt_hi[:, m - W2_TILES, :]
                dve.tensor_tensor(dst, t_bank[m % 2][:], hi.bitcast(F32), ALU.subtract).then_inc(t_free, 1)

            def finish(n):
                dve.wait_ge(down_full, n + 1)
                dve.tensor_tensor(x_sb[:, n, :], down_bank[n % TT][:, 0:D], x_sb[:, n, :],
                                  ALU.add).then_inc(out_done, 1)

            def fill(*lists):
                for items in lists:
                    for item in items:
                        if item[0] == "X":
                            low_x(*item[1:])
                        elif item[0] == "V":
                            low_v(*item[1:])
                        else:
                            rotate(item)

            for t in range(TT):
                tile_stats(0, t)
            norm_variance(0)
            norm_apply(0, range(TT))
            low_weights(0)
            low_x(0, 0)
            low_x(0, 1)
            low_weights(1)
            low_weights(2)
            dve.wait_ge(tables_loaded, 48)
            fill(START[2:5])
            low_weights(3)
            fill(START[5:])
            mask(0, S_FIRST0)
            mask(0, S_SECOND)
            low_p(0, S_FIRST0)
            low_p(0, S_SECOND)
            for u in range(UNITS):
                if u:
                    mask(u, S_FIRST0)
                    mask(u, S_SECOND)
                    fill(key(u - 1) + turned(u - 1))
                    low_p(u, S_FIRST0)
                    low_o(u - 1, 1)
                    low_p(u, S_SECOND)
                fill(values(u)[:1])
                mask(u, S_FIRST1)
                if u == PAIRS + 1:
                    add_attention(0, 1)
                fill(values(u)[1:2] + queries(u))
                if u in (UNITS - 2, UNITS - 1):
                    hidden(u - UNITS + 2)
                fill(values(u)[2:3])
                low_o(u, 0)
                if u == PAIRS:
                    add_attention(0, 0)
                fill(values(u)[3:])
                if unit_chunk(u) is not None:
                    low_weights(unit_chunk(u))
                i, p = u // PAIRS + 1, u % PAIRS
                for t in ((0,), (1, 2), (3,))[p] if p < 3 else ():
                    tile_stats(i, t)
                if p == 2:
                    norm_variance(i)
                if p == 3:
                    norm_apply(i, range(1))
                if p == 4:
                    norm_apply(i, range(1, TT))
            low_hid(0)
            low_hid(1)
            low_w2(0)
            hidden(2)
            low_o(UNITS - 1, 1)
            add_attention(1, 0)
            low_hid(2)
            hidden(3)
            low_hid(3)
            add_attention(1, 1)
            for t in range(TT):
                tile_stats(3, t)
            norm_variance(3)
            hidden(4)
            low_w2(1)
            low_hid(4)
            low_t(0)
            low_t(1)
            hidden(5)
            low_hid(5)
            norm_apply(3, range(TT))
            hidden(6)
            low_t(2)
            low_t(3)
            low_hid(6)
            hidden(7)
            low_hid(7)
            low_t(4)
            low_t(5)
            for n in range(TT):
                finish(n)
            for n in range(HT, 2 * HT):
                hidden(n)
                low_hid(n)
            for n in range(TT, 2 * TT):
                finish(n)


def tables():
    f = np.float32
    inv_freq = f(1.0) / f(10000.0) ** (np.arange(0, P, 2, dtype=f) / f(P))
    angle = (np.arange(SEQ, dtype=f)[None, :] * inv_freq[:, None]).astype(f).astype(np.float64)
    cos = np.concatenate([np.cos(angle)] * 2).astype(f)
    sin = np.concatenate([-np.sin(angle), np.sin(angle)]).astype(f)
    lam = np.exp2(f(-8.0) * np.arange(1, HEADS + 1, dtype=f) / f(HEADS)).astype(np.float64)
    lag = np.arange(SEQ)[None, :] - np.arange(P)[:, None]
    decay = np.where(lag[:, None, :] >= 0, np.exp(-lam[None, :, None] * np.maximum(lag, 0)[:, None, :]), 0.0)
    decay = decay.astype(f).reshape(P, 4, 4, SEQ).transpose(1, 0, 2, 3)
    signs = np.array([[-1.0 if bin(i & j).count("1") % 2 else 1.0 for j in range(P)] for i in range(P)])
    return {"cos": cos, "sin": sin, "decay": decay, "ident": np.eye(P, dtype=f),
            "hadamard": (signs / np.sqrt(HID)).astype(f)}


def layouts(x, wq, wk, wv, wo, w1, w2, w3):
    def stationary(w):
        r = w.reshape(-1, 4, P, KD, P).transpose(0, 4, 1, 3, 2)
        return r.reshape(-1, P, 4 * KD * P)
    return {
        "x": x.reshape(NSEQ, 2, P, D).transpose(0, 2, 1, 3),
        "wk": stationary(wk),
        "wv": wv.reshape(1, KVH * P, KD, P).transpose(0, 3, 2, 1).reshape(1, P, CH),
        "wq": stationary(wq),
        "wo": wo.reshape(D, 4, 4, P).transpose(1, 3, 2, 0).reshape(4, P, CH),
        "w1": stationary(w1),
        "w3": stationary(w3),
        "w2": w2.reshape(2, P, HT, P).transpose(0, 3, 2, 1).reshape(2, P, CH),
    }


def kernel(L0_attn_x, L0_attn_wq, L0_attn_wk, L0_attn_wv, L0_attn_wo, L0_ffn_W1, L0_ffn_W2, L0_ffn_W3):
    import concourse.bacc as bacc
    from concourse.bass_utils import run_bass_kernel_spmd

    laid = layouts(*(np.asarray(a) for a in (L0_attn_x, L0_attn_wq, L0_attn_wk, L0_attn_wv, L0_attn_wo,
                                              L0_ffn_W1, L0_ffn_W2, L0_ffn_W3)))
    laid.update(tables())
    nc = bacc.Bacc("TRN2", target_bir_lowering=False, num_devices=1)
    arrays, args = {}, {}
    for name, a in laid.items():
        a = np.ascontiguousarray(a)
        arrays[f"in_{name}"] = a
        args[name] = nc.dram_tensor(f"in_{name}", a.shape, mybir.dt.from_np(a.dtype), kind="ExternalInput").ap()
    out = nc.dram_tensor("out", (HALVES * TT, P, D), F32, kind="ExternalOutput").ap()
    build(nc, out=out, **args)
    r = run_bass_kernel_spmd(nc, [arrays], core_ids=[0])
    return r.results[0]["out"].reshape(NSEQ, SEQ, D)
```
